# Optimizing a Trainium2 kernel written in Bass

```python
import numpy as np
import jax
import jax.numpy as jnp

def _softmax(x, axis=-1):
    return jax.nn.softmax(x, axis=axis)

def _gelu(x):
    return jax.nn.gelu(x, approximate=True)

def _silu(x):
    return jax.nn.silu(x)

def _sigmoid(x):
    return jax.nn.sigmoid(x)

def _layernorm(x, axis=-1, eps=1e-05):
    m = jnp.mean(x, axis=axis, keepdims=True)
    v = jnp.var(x, axis=axis, keepdims=True)
    return (x - m) / jnp.sqrt(v + eps)

def _scatter_add(tgt, idx, src, axis=0):
    return tgt.at[idx].add(src)

def _segment_sum(src, seg, n):
    return jax.ops.segment_sum(src, seg, n)
kernel_name = 'mk_gnn_resnorm_d4_gnn_r32_e75f35'

def setup_inputs(seed: int=0):
    np.random.seed(seed)
    _w = jnp.asarray

    def _rec_inputs():
        import jax
        import jax.numpy as jnp
        _gk = jax.random.key(seed)
        x = -0.001003 + 1 * jax.random.normal(jax.random.fold_in(_gk, 1), (64, 768), jnp.float32)
        src = jax.random.randint(jax.random.fold_in(_gk, 2), (1024,), 0, 64, jnp.int32)
        dst = jax.random.randint(jax.random.fold_in(_gk, 3), (1024,), 0, 64, jnp.int32)
        _o = jnp.argsort(dst, stable=True)
        src = src[_o]
        dst = dst[_o]
        edge_type_3 = jax.random.randint(jax.random.fold_in(_gk, 12), (1024,), 0, 3, jnp.int32)
        return (x, src, dst, edge_type_3)
    x, src, dst, edge_type_3 = _rec_inputs()

    def _L0_gnn_setup():
        import jax, jax.numpy as jnp
        import numpy as np
        NUM_RELATIONS = 3

        def _rgcn(x, W_rel, W_root, bias, src, dst, etype):
            n = x.shape[0]
            xr = jnp.einsum('ni,rio->rno', x, W_rel)
            msg = xr[etype, src]
            out = x @ W_root + bias
            for r in range(NUM_RELATIONS):
                m = etype == r
                s = jax.ops.segment_sum(jnp.where(m[:, None], msg, 0.0), dst, num_segments=n)
                c = jax.ops.segment_sum(m.astype(x.dtype), dst, num_segments=n)
                out = out + s / jnp.maximum(c, 1.0)[:, None]
            return out

        def _gate(h, q, Wg, bg, Wq, bq):
            B, L, F = q.shape
            N = h.shape[0] // B
            h3 = h.reshape(B, N, F)
            hg = jnp.einsum('bnf,gf->bng', h3, Wg[:, :F])
            qg = jnp.einsum('blf,gf->blg', q, Wg[:, F:]) + bg
            attn = jax.nn.sigmoid(hg[:, :, None, :] + qg[:, None, :, :])
            qi = jnp.einsum('bnlf,blf->bnf', attn, q)
            alpha = jax.nn.sigmoid(jnp.einsum('bnf,gf->bng', h3, Wq[:, :F]) + jnp.einsum('bnf,gf->bng', qi, Wq[:, F:]) + bq)
            hn = alpha * jnp.tanh(qi) + (1.0 - alpha) * h3
            return hn.reshape(B * N, F)
        key = jax.random.key(seed)
        ks = jax.random.split(key, 16)
        F = 768
        BN, E, B, L = (64, 2048, 8, 64)
        s = 0.02
        return {'x': jax.random.normal(ks[0], (BN, F), jnp.float32), 'edge_index': jax.random.randint(ks[1], (2, E), 0, BN), 'edge_type': jax.random.randint(ks[2], (E,), 0, NUM_RELATIONS), 'query_embs': jax.random.normal(ks[3], (B, L, F), jnp.float32), 'W_rel1': jax.random.normal(ks[4], (NUM_RELATIONS, F, F), jnp.float32) * s, 'W_root1': jax.random.normal(ks[5], (F, F), jnp.float32) * s, 'b1': jnp.zeros((F,), jnp.float32), 'W_rel2': jax.random.normal(ks[6], (NUM_RELATIONS, F, F), jnp.float32) * s, 'W_root2': jax.random.normal(ks[7], (F, F), jnp.float32) * s, 'b2': jnp.zeros((F,), jnp.float32), 'Wg': jax.random.normal(ks[8], (F, 2 * F), jnp.float32) * s, 'bg': jnp.zeros((F,), jnp.float32), 'Wq': jax.random.normal(ks[9], (F, 2 * F), jnp.float32) * s, 'bq': jnp.zeros((F,), jnp.float32)}
    _L0_gnn_all = _L0_gnn_setup()
    _L0_gnn_in = {k: v for k, v in _L0_gnn_all.items() if k in ('query_embs', 'W_rel1', 'W_root1', 'b1', 'W_rel2', 'W_root2', 'b2', 'Wg', 'bg', 'Wq', 'bq')}
    del _L0_gnn_all

    def _L1_gnn_setup():
        import jax, jax.numpy as jnp
        import numpy as np
        N_NODES = 10000
        N_EDGES = 3125
        DIM = 768
        key = jax.random.key(seed)
        k1, k2, k3, k4 = jax.random.split(key, 4)
        x = jax.random.normal(k1, (N_NODES, DIM), dtype=jnp.float32)
        edge_index = jax.random.randint(k2, (2, N_EDGES), 0, N_NODES, dtype=jnp.int32)
        W = jax.random.normal(k3, (DIM, DIM), dtype=jnp.float32) / np.sqrt(DIM)
        b = jnp.zeros((DIM,), dtype=jnp.float32)
        return {'x': x, 'edge_index': edge_index, 'W': W, 'b': b}
    _L1_gnn_all = _L1_gnn_setup()
    _L1_gnn_in = {k: v for k, v in _L1_gnn_all.items() if k in ('W', 'b')}
    del _L1_gnn_all

    def _L2_gnn_setup():
        import jax, jax.numpy as jnp
        import numpy as np
        NEG_SLOPE = 0.2
        EPS = 1e-16
        N_NODES = 1024
        N_EDGES = 5000
        DIM = 768
        HEADS1 = 4
        OUT1 = DIM // HEADS1
        HEADS2 = 1
        OUT2 = DIM
        N_REL = 3

        def rgat_conv(x, W, q, k, b, src, dst, etype, heads, out_ch, n_nodes):
            xr = jnp.einsum('nd,rdf->rnf', x, W)
            oi = xr[etype, dst]
            oj = xr[etype, src]
            qi = oi @ q
            kj = oj @ k
            alpha = jax.nn.leaky_relu(qi + kj, NEG_SLOPE)
            m = jax.ops.segment_max(alpha, dst, num_segments=n_nodes)
            e = jnp.exp(alpha - m[dst])
            z = jax.ops.segment_sum(e, dst, num_segments=n_nodes)
            a = e / (z[dst] + EPS)
            msg = (a[:, :, None] * oj.reshape(-1, heads, out_ch)).reshape(-1, heads * out_ch)
            out = jax.ops.segment_sum(msg, dst, num_segments=n_nodes)
            return out + b
        key = jax.random.key(seed)
        ks = jax.random.split(key, 12)
        s = 0.02
        return {'x': jax.random.normal(ks[0], (N_NODES, DIM), dtype=jnp.float32), 'edge_index': jax.random.randint(ks[1], (2, N_EDGES), 0, N_NODES, dtype=jnp.int64), 'edge_type': jax.random.randint(ks[2], (N_EDGES,), 0, N_REL, dtype=jnp.int64), 'W1': jax.random.normal(ks[3], (N_REL, DIM, HEADS1 * OUT1), dtype=jnp.float32) * s, 'q1': jax.random.normal(ks[4], (HEADS1 * OUT1, HEADS1), dtype=jnp.float32) * s, 'k1': jax.random.normal(ks[5], (HEADS1 * OUT1, HEADS1), dtype=jnp.float32) * s, 'b1': jnp.zeros((HEADS1 * OUT1,), dtype=jnp.float32), 'W2': jax.random.normal(ks[6], (N_REL, DIM, HEADS2 * OUT2), dtype=jnp.float32) * s, 'q2': jax.random.normal(ks[7], (HEADS2 * OUT2, HEADS2), dtype=jnp.float32) * s, 'k2': jax.random.normal(ks[8], (HEADS2 * OUT2, HEADS2), dtype=jnp.float32) * s, 'b2': jnp.zeros((HEADS2 * OUT2,), dtype=jnp.float32)}
    _L2_gnn_all = _L2_gnn_setup()
    _L2_gnn_in = {k: v for k, v in _L2_gnn_all.items() if k in ('W1', 'q1', 'k1', 'b1', 'W2', 'q2', 'k2', 'b2')}
    del _L2_gnn_all

    def _L3_gnn_setup():
        import jax, jax.numpy as jnp
        import numpy as np
        N_NODES = 10000
        D = 768
        N_EDGES = 5000

        def gcn_conv(x, W, b, src, dst, n_nodes):
            h = x @ W
            deg = jax.ops.segment_sum(jnp.ones_like(dst, dtype=h.dtype), dst, num_segments=n_nodes)
            dinv = jnp.where(deg > 0, jax.lax.rsqrt(deg), 0.0)
            norm = dinv[src] * dinv[dst]
            msgs = h[src] * norm[:, None]
            out = jax.ops.segment_sum(msgs, dst, num_segments=n_nodes)
            return out + b

        def add_self_loops(edge_index, n_nodes):
            loop = jnp.arange(n_nodes, dtype=edge_index.dtype)
            src = jnp.concatenate([edge_index[0], loop])
            dst = jnp.concatenate([edge_index[1], loop])
            return (src, dst)
        key = jax.random.key(seed)
        k1, k2, k3, k4 = jax.random.split(key, 4)
        x = jax.random.normal(k1, (N_NODES, D), dtype=jnp.float32)
        edge_index = jax.random.randint(k2, (2, N_EDGES), 0, N_NODES, dtype=jnp.int32)
        glorot = float(np.sqrt(6.0 / (D + D)))
        W1 = jax.random.uniform(k3, (D, D), jnp.float32, -glorot, glorot)
        W2 = jax.random.uniform(k4, (D, D), jnp.float32, -glorot, glorot)
        b1 = jnp.zeros((D,), jnp.float32)
        b2 = jnp.zeros((D,), jnp.float32)
        return {'x': x, 'W1': W1, 'b1': b1, 'W2': W2, 'b2': b2, 'edge_index': edge_index}
    _L3_gnn_all = _L3_gnn_setup()
    _L3_gnn_in = {k: v for k, v in _L3_gnn_all.items() if k in ('W1', 'b1', 'W2', 'b2')}
    del _L3_gnn_all
    return {'x': x, 'src': src, 'dst': dst, 'edge_type_3': edge_type_3, 'L0_gnn_query_embs': _L0_gnn_in['query_embs'], 'L0_gnn_W_rel1': _L0_gnn_in['W_rel1'], 'L0_gnn_W_root1': _L0_gnn_in['W_root1'], 'L0_gnn_b1': _L0_gnn_in['b1'], 'L0_gnn_W_rel2': _L0_gnn_in['W_rel2'], 'L0_gnn_W_root2': _L0_gnn_in['W_root2'], 'L0_gnn_b2': _L0_gnn_in['b2'], 'L0_gnn_Wg': _L0_gnn_in['Wg'], 'L0_gnn_bg': _L0_gnn_in['bg'], 'L0_gnn_Wq': _L0_gnn_in['Wq'], 'L0_gnn_bq': _L0_gnn_in['bq'], 'L1_gnn_W': _L1_gnn_in['W'], 'L1_gnn_b': _L1_gnn_in['b'], 'L2_gnn_W1': _L2_gnn_in['W1'], 'L2_gnn_q1': _L2_gnn_in['q1'], 'L2_gnn_k1': _L2_gnn_in['k1'], 'L2_gnn_b1': _L2_gnn_in['b1'], 'L2_gnn_W2': _L2_gnn_in['W2'], 'L2_gnn_q2': _L2_gnn_in['q2'], 'L2_gnn_k2': _L2_gnn_in['k2'], 'L2_gnn_b2': _L2_gnn_in['b2'], 'L3_gnn_W1': _L3_gnn_in['W1'], 'L3_gnn_b1': _L3_gnn_in['b1'], 'L3_gnn_W2': _L3_gnn_in['W2'], 'L3_gnn_b2': _L3_gnn_in['b2']}

def reference(x, src, dst, edge_type_3, L0_gnn_query_embs, L0_gnn_W_rel1, L0_gnn_W_root1, L0_gnn_b1, L0_gnn_W_rel2, L0_gnn_W_root2, L0_gnn_b2, L0_gnn_Wg, L0_gnn_bg, L0_gnn_Wq, L0_gnn_bq, L1_gnn_W, L1_gnn_b, L2_gnn_W1, L2_gnn_q1, L2_gnn_k1, L2_gnn_b1, L2_gnn_W2, L2_gnn_q2, L2_gnn_k2, L2_gnn_b2, L3_gnn_W1, L3_gnn_b1, L3_gnn_W2, L3_gnn_b2):
    import jax
    import jax.numpy as jnp

    def _L0_gnn_ref(x, edge_index, edge_type, query_embs, W_rel1, W_root1, b1, W_rel2, W_root2, b2, Wg, bg, Wq, bq):
        import jax, jax.numpy as jnp
        import numpy as np
        NUM_RELATIONS = 3

        def _rgcn(x, W_rel, W_root, bias, src, dst, etype):
            n = x.shape[0]
            xr = jnp.einsum('ni,rio->rno', x, W_rel)
            msg = xr[etype, src]
            out = x @ W_root + bias
            for r in range(NUM_RELATIONS):
                m = etype == r
                s = jax.ops.segment_sum(jnp.where(m[:, None], msg, 0.0), dst, num_segments=n)
                c = jax.ops.segment_sum(m.astype(x.dtype), dst, num_segments=n)
                out = out + s / jnp.maximum(c, 1.0)[:, None]
            return out

        def _gate(h, q, Wg, bg, Wq, bq):
            B, L, F = q.shape
            N = h.shape[0] // B
            h3 = h.reshape(B, N, F)
            hg = jnp.einsum('bnf,gf->bng', h3, Wg[:, :F])
            qg = jnp.einsum('blf,gf->blg', q, Wg[:, F:]) + bg
            attn = jax.nn.sigmoid(hg[:, :, None, :] + qg[:, None, :, :])
            qi = jnp.einsum('bnlf,blf->bnf', attn, q)
            alpha = jax.nn.sigmoid(jnp.einsum('bnf,gf->bng', h3, Wq[:, :F]) + jnp.einsum('bnf,gf->bng', qi, Wq[:, F:]) + bq)
            hn = alpha * jnp.tanh(qi) + (1.0 - alpha) * h3
            return hn.reshape(B * N, F)
        src, dst = (edge_index[0], edge_index[1])
        h = jax.nn.relu(_rgcn(x, W_rel1, W_root1, b1, src, dst, edge_type))
        h = _gate(h, query_embs, Wg, bg, Wq, bq)
        h = jax.nn.relu(_rgcn(h, W_rel2, W_root2, b2, src, dst, edge_type))
        h = _gate(h, query_embs, Wg, bg, Wq, bq)
        return h

    def _L1_gnn_ref(x, edge_index, W, b):
        import jax, jax.numpy as jnp
        import numpy as np
        N_NODES = 10000
        N_EDGES = 3125
        DIM = 768
        n = x.shape[0]
        loop = jnp.arange(n, dtype=edge_index.dtype)
        src = jnp.concatenate([edge_index[0], loop])
        dst = jnp.concatenate([edge_index[1], loop])
        deg = jax.ops.segment_sum(jnp.ones_like(dst, dtype=x.dtype), dst, num_segments=n)
        deg_inv_sqrt = jnp.where(deg > 0, jax.lax.rsqrt(deg), 0.0)
        norm = deg_inv_sqrt[src] * deg_inv_sqrt[dst]
        h = x @ W
        msg = h[src] * norm[:, None]
        out = jax.ops.segment_sum(msg, dst, num_segments=n)
        return out + b

    def _L2_gnn_ref(x, edge_index, edge_type, W1, q1, k1, b1, W2, q2, k2, b2):
        import jax, jax.numpy as jnp
        import numpy as np
        NEG_SLOPE = 0.2
        EPS = 1e-16
        N_NODES = 1024
        N_EDGES = 5000
        DIM = 768
        HEADS1 = 4
        OUT1 = DIM // HEADS1
        HEADS2 = 1
        OUT2 = DIM
        N_REL = 3

        def rgat_conv(x, W, q, k, b, src, dst, etype, heads, out_ch, n_nodes):
            xr = jnp.einsum('nd,rdf->rnf', x, W)
            oi = xr[etype, dst]
            oj = xr[etype, src]
            qi = oi @ q
            kj = oj @ k
            alpha = jax.nn.leaky_relu(qi + kj, NEG_SLOPE)
            m = jax.ops.segment_max(alpha, dst, num_segments=n_nodes)
            e = jnp.exp(alpha - m[dst])
            z = jax.ops.segment_sum(e, dst, num_segments=n_nodes)
            a = e / (z[dst] + EPS)
            msg = (a[:, :, None] * oj.reshape(-1, heads, out_ch)).reshape(-1, heads * out_ch)
            out = jax.ops.segment_sum(msg, dst, num_segments=n_nodes)
            return out + b
        src, dst = (edge_index[0], edge_index[1])
        n = x.shape[0]
        h = rgat_conv(x, W1, q1, k1, b1, src, dst, edge_type, HEADS1, OUT1, n)
        h = jax.nn.elu(h)
        out = rgat_conv(h, W2, q2, k2, b2, src, dst, edge_type, HEADS2, OUT2, n)
        return out

    def _L3_gnn_ref(x, W1, b1, W2, b2, edge_index):
        import jax, jax.numpy as jnp
        import numpy as np
        N_NODES = 10000
        D = 768
        N_EDGES = 5000

        def gcn_conv(x, W, b, src, dst, n_nodes):
            h = x @ W
            deg = jax.ops.segment_sum(jnp.ones_like(dst, dtype=h.dtype), dst, num_segments=n_nodes)
            dinv = jnp.where(deg > 0, jax.lax.rsqrt(deg), 0.0)
            norm = dinv[src] * dinv[dst]
            msgs = h[src] * norm[:, None]
            out = jax.ops.segment_sum(msgs, dst, num_segments=n_nodes)
            return out + b

        def add_self_loops(edge_index, n_nodes):
            loop = jnp.arange(n_nodes, dtype=edge_index.dtype)
            src = jnp.concatenate([edge_index[0], loop])
            dst = jnp.concatenate([edge_index[1], loop])
            return (src, dst)
        n = x.shape[0]
        src, dst = add_self_loops(edge_index, n)
        h = gcn_conv(x, W1, b1, src, dst, n)
        h = jax.nn.relu(h)
        out = gcn_conv(h, W2, b2, src, dst, n)
        return out
    edge_index = jnp.stack([src, dst])
    x = _layernorm(x + _L0_gnn_ref(x, edge_index, edge_type_3, L0_gnn_query_embs, L0_gnn_W_rel1, L0_gnn_W_root1, L0_gnn_b1, L0_gnn_W_rel2, L0_gnn_W_root2, L0_gnn_b2, L0_gnn_Wg, L0_gnn_bg, L0_gnn_Wq, L0_gnn_bq), axis=-1)
    x = _layernorm(x + _L1_gnn_ref(x, edge_index, L1_gnn_W, L1_gnn_b), axis=-1)
    x = _layernorm(x + _L2_gnn_ref(x, edge_index, edge_type_3, L2_gnn_W1, L2_gnn_q1, L2_gnn_k1, L2_gnn_b1, L2_gnn_W2, L2_gnn_q2, L2_gnn_k2, L2_gnn_b2), axis=-1)
    x = _layernorm(x + _L3_gnn_ref(x, L3_gnn_W1, L3_gnn_b1, L3_gnn_W2, L3_gnn_b2, edge_index), axis=-1)
    return x

_drawn_inputs = setup_inputs


def setup_inputs(seed=0):
    import zlib

    import numpy as np

    out = dict(_drawn_inputs(seed))
    spreads = {'L0_gnn_b1': (0.0, 0.525),
     'L0_gnn_b2': (0.0, 0.1),
     'L0_gnn_bg': (0.0, 0.433),
     'L0_gnn_bq': (0.0, 0.527),
     'L1_gnn_b': (0.0, 0.1),
     'L2_gnn_b1': (0.0, 0.1),
     'L2_gnn_b2': (0.0, 0.1),
     'L3_gnn_b1': (0.0, 0.1),
     'L3_gnn_b2': (0.0, 0.1)}
    factors = {'L2_gnn_q1': 8.0, 'L2_gnn_k1': 8.0, 'L2_gnn_q2': 8.0, 'L2_gnn_k2': 8.0}
    for name, (base, spread) in spreads.items():
        noise = np.random.default_rng([zlib.crc32(name.encode()), seed]).standard_normal(out[name].shape)
        drawn = base * np.exp(spread * noise) if base else spread * noise
        out[name] = jnp.asarray(drawn.astype(out[name].dtype))
    for name, factor in factors.items():
        out[name] = (out[name] * factor).astype(out[name].dtype)
    return out
```

```python
from contextlib import ExitStack

import concourse.bass as bass
from concourse import mybir

ALU = mybir.AluOpType
ACT = mybir.ActivationFunctionType
AX = mybir.AxisListType
F32 = mybir.dt.float32
BF16 = mybir.dt.bfloat16
I32 = mybir.dt.int32

P = 128
NEG = -1.0e30
LN_EPS = 1e-5
SOFTMAX_EPS = 1e-16
SLOPE = 0.2


def gnn_kernel(nc: bass.Bass, a, out):
    N, D = a["x"].shape
    E = a["src"].shape[0]
    R = a["L0_gnn_W_rel1"].shape[0]
    B, L, _ = a["L0_gnn_query_embs"].shape
    NB = N // B
    HD = D // 2
    KC = D // P
    JC = KC // 2
    EC = E // P
    NP = B // 2
    TILES = NP * NB
    GN = 32
    PPG = GN // (2 * NB)
    assert N == 64 and 2 * L == P and 2 * HD == D and KC % 2 == 0


    PLAN = [("Wg_q", 0, 2), ("Wg_h", 3, 2), ("rel1_0", 5, 1), ("rel1_1", 6, 1), ("rel1_2", 0, 1), ("root1", 3, 1),
            ("Wq_h", 5, 2), ("Wq_q", 6, 2), ("rel2_0", 3, 1), ("rel2_1", 2, 1), ("rel2_2", 5, 1), ("root2", 6, 1),
            ("L1_W", 3, 1), ("L2_W1_0", 2, 1), ("L2_W1_1", 5, 1), ("L2_W1_2", 6, 1),
            ("L2_W2_0", 4, 1), ("L2_W2_1", 0, 1), ("L2_W2_2", 1, 1), ("L3_W1", 3, 1), ("L3_W2", 2, 1)]
    SLOT = {key: s for key, s, _ in PLAN}
    PARTS = {key: n for key, _, n in PLAN}

    with ExitStack() as ctx:
        def sb(name, shape, dt=F32):
            return ctx.enter_context(nc.sbuf_tensor(name, shape, dt))

        def sem(name):
            return ctx.enter_context(nc.semaphore(name))

        NSLOT = 7
        W = [sb(f"W{s}", [P, KC, D]) for s in range(NSLOT)]
        qn = sb("qn", [P, NP, D])
        qg = sb("qg", [P, NP, D])
        PRODS = 4
        prod = sb("prod", [P, PRODS, D])
        PRES = 4
        pre = sb("pre", [P, PRES, D])
        bias = sb("bias", [P, 4, HD])
        nodeT = sb("nodeT", [P, JC, P])
        adjT = sb("adjT", [P, R + 1, P])
        gcnT = sb("gcnT", [P, P])
        ident = sb("ident", [P, P])
        avg = sb("avg", [P, P])
        bsel = sb("bsel", [3 * GN, PPG * NB, P], BF16)
        i3 = sb("i3", [3 * GN, GN], BF16)
        rsel = sb("rsel", [P, P])
        stack = sb("stack", [3 * GN, 2, 2, HD], BF16)
        xa = sb("xa", [P, HD])
        hh = sb("hh", [P, HD])
        hx = sb("hx", [P, HD])
        t0 = sb("t0", [P, HD])
        t1 = sb("t1", [P, HD])
        t2 = sb("t2", [P, HD])
        hi = sb("hi", [P, HD], BF16)
        mid = sb("mid", [P, HD], BF16)
        M = sb("M", [P, R * N])
        maskb = sb("maskb", [P, R * N])
        small = sb("small", [P, 64])
        eidx = sb("eidx", [P, 3, EC], I32)
        qk = sb("qk", [P, KC, 8])
        qk2 = sb("qk2", [P, KC, 2])

        prod_f = prod[:, :, :].rearrange("p a b -> p (a b)")
        hot_src = prod_f[:, 0:EC * R * N // 2].bitcast(BF16).rearrange("p (c k) -> p c k", c=EC)
        o = EC * R * N // 2
        hot_dst = prod_f[:, o:o + EC * P // 2].bitcast(BF16).rearrange("p (c k) -> p c k", c=EC)
        o += EC * P // 2
        blockd = prod_f[:, o:o + (R + 1) * P].rearrange("p (r k) -> p r k", r=R + 1)
        mixT = prod_f[:, 0:JC * (R + 1) * P].rearrange("p (j n) -> p j n", j=JC)
        qiT = prod_f[:, JC * (R + 1) * P:JC * (R + 2) * P].rearrange("p (j n) -> p j n", j=JC)
        pre_f = pre[:, :, :].rearrange("p a b -> p (a b)")
        cols_i = pre_f[:, 0:R * N].bitcast(I32)
        cols_f = pre_f[:, R * N:2 * R * N]
        edge_f = pre_f[:, 2 * R * N:2 * R * N + 3 * EC].rearrange("p (a c) -> p a c", a=3)
        qT = W[2][:, :, 0:NP * P]
        qn_f = qn[:, :, :].rearrange("p a b -> p (a b)")
        qg_f = qg[:, :, :].rearrange("p a b -> p (a b)")
        X01 = qn_f[:, 0:D]
        X2 = qn_f[0:N, D:2 * D]
        XT = qn_f[:, 2 * D:2 * D + KC * R * N].rearrange("p (k n) -> p k n", k=KC)
        score = qg_f[:, 0:HD]
        leaky = qg_f[:, HD:2 * HD]
        expd = qg_f[:, 2 * HD:3 * HD]
        wts = qg_f[:, 3 * HD:4 * HD]
        wT1 = qg_f[:, 4 * HD:4 * HD + 2 * P]
        wT2 = qg_f[0:N, 4 * HD + 2 * P:4 * HD + 4 * P]
        QKT = qg_f[0:8, 6 * HD:6 * HD + R * N]

        ps = ctx.enter_context(nc.psum_tensor("ps", [P, 8, 512], F32))
        RING = 2
        GATE, ACC, TRB = 4, 6, 7

        def ring(t):
            s = 2 * (t % RING)
            return ps[:, s:s + 2, 0:HD]

        def by_half(tile):
            return tile.rearrange("p (h f) -> p h f", h=2)

        loaded = {key: [sem(f"{key}_{c}_loaded") for c in range(n)] for key, _, n in PLAN}
        edges_loaded = sem("edges_loaded")
        x_loaded = sem("x_loaded")
        q_loaded = sem("q_loaded")
        qk_loaded = sem("qk_loaded")
        bias_loaded = [sem(f"bias{s}_loaded") for s in range(4)]
        out_stored = sem("out_stored")
        pool_chain = sem("pool_chain")
        vec_chain = sem("vec_chain")
        act_chain = sem("act_chain")
        ident_ready = sem("ident_ready")
        consts_ready = sem("consts_ready")
        hot_ready = sem("hot_ready")
        counts_done = sem("counts_done")
        blocks_ready = sem("blocks_ready")
        adj_turned = sem("adj_turned")
        adj_ready = sem("adj_ready")
        deg_ready = sem("deg_ready")
        sqrt_deg = sem("sqrt_deg")
        turned = sem("turned")
        turned_out_v = sem("turned_out_v")
        turned_out_s = sem("turned_out_s")
        qg_done = sem("qg_done")
        qg_out_v = sem("qg_out_v")
        qg_out_s = sem("qg_out_s")
        mixed = sem("mixed")
        mix_out_v = sem("mix_out_v")
        mix_out_s = sem("mix_out_s")
        rgcn_done = sem("rgcn_done")
        h_ready = sem("h_ready")
        node_turned = sem("node_turned")
        nodeT_ready = sem("nodeT_ready")
        hg_done = sem("hg_done")
        hi_ready = sem("hi_ready")
        mid_ready = sem("mid_ready")
        hi_stacked = sem("hi_stacked")
        mid_stacked = sem("mid_stacked")
        lo_stacked = sem("lo_stacked")
        hg_cast = sem("hg_cast")
        pre_ready = sem("pre_ready")
        sig_ready = sem("sig_ready")
        prod_v = sem("prod_v")
        prod_p = sem("prod_p")
        reduced = sem("reduced")
        qi_ready = sem("qi_ready")
        tanh_ready = sem("tanh_ready")
        qi_turned = sem("qi_turned")
        qiT_ready = sem("qiT_ready")
        alpha_done = sem("alpha_done")
        alpha_pre = sem("alpha_pre")
        alpha_ready = sem("alpha_ready")
        x_ready = sem("x_ready")
        ln_parts = sem("ln_parts")
        ln_mean = sem("ln_mean")
        ln_var = sem("ln_var")
        ln_std = sem("ln_std")
        proj_done = sem("proj_done")
        rel_done = sem("rel_done")
        X_out_v = sem("X_out_v")
        X_out_s = sem("X_out_s")
        X_turned = sem("X_turned")
        XT_out_v = sem("XT_out_v")
        XT_out_s = sem("XT_out_s")
        qk_done = sem("qk_done")
        qkT_ready = sem("qkT_ready")
        score_done = sem("score_done")
        shifted = sem("shifted")
        exp_ready = sem("exp_ready")
        wts_ready = sem("wts_ready")
        wts_turned = sem("wts_turned")
        wT_out_v = sem("wT_out_v")
        wT_out_s = sem("wT_out_s")
        att_done = sem("att_done")
        elu_min = sem("elu_min")
        elu_exp = sem("elu_exp")
        y_ready = sem("y_ready")

        POOL_NODES = (0, 2, 3, 5, 6)

        def on_pool(T):
            return T % NB in POOL_NODES

        def pool_tiles(T):
            return sum(on_pool(k) for k in range(T))

        def vec_tiles(T):
            return T - pool_tiles(T)

        GROUPS = 2 * KC

        def group_on_act(g):
            return g >= G_QH or g % 2 == 0

        G_Q = GROUPS
        NQG = KC
        G_H = G_Q + NQG
        G_QH = G_H + GROUPS
        G_END = G_QH + 2 * GROUPS

        def act_groups(g):
            return sum(group_on_act(k) for k in range(g))

        def vec_groups(g):
            return g - act_groups(g)

        def wait_group_out(eng, g):
            if group_on_act(g):
                eng.wait_ge(turned_out_s, act_groups(g + 1))
            else:
                eng.wait_ge(turned_out_v, vec_groups(g + 1))

        def wait_groups_out(eng, g):
            if act_groups(g):
                eng.wait_ge(turned_out_s, act_groups(g))
            if vec_groups(g):
                eng.wait_ge(turned_out_v, vec_groups(g))

        EARLY = (0, 1, 2, 5, 6, 7)
        LATE = 2 * GROUPS - len(EARLY)

        def late_groups(t):
            return len(EARLY) + t * LATE // TILES

        def group_bank(g):
            if g < G_QH:
                return 4 + g % 4
            return EARLY[g - G_QH] if g - G_QH < len(EARLY) else TRB

        UNITS = 2 * NP

        def unit_bank(u):
            return u % 4 if u < UNITS - 1 else GATE + 1

        def wait_units_out(eng, u):
            eng.wait_ge(qg_out_v, (u + 1) // 2)
            eng.wait_ge(qg_out_s, u // 2)

        WgT_q, WgT_h, WqT_h, WqT_q = W[1], W[4], W[0], W[1]

        def group_dst(g):
            if g < G_Q:
                return WgT_q[:, g % KC, (g // KC) * HD:(g // KC + 1) * HD], HD
            if g < G_H:
                return qT[:, g - G_Q, :], NP * P
            if g < G_QH:
                k = g - G_H
                return WgT_h[:, k % KC, (k // KC) * HD:(k // KC + 1) * HD], HD
            k = (g - G_QH) % GROUPS
            dst = WqT_h if g - G_QH < GROUPS else WqT_q
            return dst[:, k % KC, (k // KC) * HD:(k // KC + 1) * HD], HD

        def copy_group(eng, g, done):
            dst, n = group_dst(g)
            eng.wait_ge(turned, g + 1)
            src = ps[:, group_bank(g), 0:n]
            ins = nc.vector.tensor_copy(dst, src) if done is turned_out_v else nc.scalar.copy(dst, src)
            ins.then_inc(done, 1)

        def wait_loaded(eng, key, part=0):
            eng.wait_ge(loaded[key][part], 16)

        def halves(dram):
            return dram.rearrange("(k p) n -> p k n", p=P)

        block = ctx.enter_context(nc.Block())

        @block.sync
        def _(sp):
            def load(key, dram, after=None, value=0):
                if after is not None:
                    sp.wait_ge(after, value)
                s = SLOT[key]
                n = KC // PARTS[key]
                v = halves(dram)
                for c in range(PARTS[key]):
                    sp.dma_start(W[s][:, c * n:(c + 1) * n, :], v[:, c * n:(c + 1) * n, :]).then_inc(loaded[key][c], 16)

            def load_bias(s, dram, after=None, value=0):
                if after is not None:
                    sp.wait_ge(after, value)
                for h in range(2):
                    sp.dma_start(bias[h * N:(h + 1) * N, s, :],
                                 dram[h * HD:(h + 1) * HD].partition_broadcast(N)).then_inc(bias_loaded[s], 16)

            for i, name in enumerate(("src", "dst", "edge_type_3")):
                sp.dma_start(eidx[:, i, :], a[name].rearrange("(p c) -> p c", p=P)).then_inc(edges_loaded, 16)
            Wg, Wq = a["L0_gnn_Wg"], a["L0_gnn_Wq"]
            load("Wg_q", Wg[:, D:2 * D])
            for b in range(2):
                sp.dma_start(qn[b * L:(b + 1) * L, :, :],
                             a["L0_gnn_query_embs"].rearrange("(p b) l f -> b l p f", b=2)[b]).then_inc(q_loaded, 16)
            load("Wg_h", Wg[:, 0:D])
            for h in range(2):
                sp.dma_start(xa[h * N:(h + 1) * N, :], a["x"][:, h * HD:(h + 1) * HD]).then_inc(x_loaded, 16)
            load("rel1_0", a["L0_gnn_W_rel1"][0])
            load("rel1_1", a["L0_gnn_W_rel1"][1])
            for s, name in enumerate(("b1", "b2", "bg", "bq")):
                load_bias(s, a[f"L0_gnn_{name}"])
            load("rel1_2", a["L0_gnn_W_rel1"][2], turned, GROUPS)
            load("root1", a["L0_gnn_W_root1"], turned, G_QH)
            load("Wq_h", Wq[:, 0:D], rgcn_done, 1)
            load("Wq_q", Wq[:, D:2 * D], rgcn_done, 2)
            load("rel2_0", a["L0_gnn_W_rel2"][0], rgcn_done, R + 1)
            load("rel2_1", a["L0_gnn_W_rel2"][1], qg_done, UNITS)
            load("rel2_2", a["L0_gnn_W_rel2"][2], turned, G_QH + GROUPS)
            load("root2", a["L0_gnn_W_root2"], turned, G_END)
            for q, name in enumerate(("q", "k")):
                sp.dma_start(qk[:, :, 4 * q:4 * q + 4], halves(a[f"L2_gnn_{name}1"]),
                             allow_slow_non_contiguous=True).then_inc(qk_loaded, 16)
                sp.dma_start(qk2[:, :, q:q + 1], halves(a[f"L2_gnn_{name}2"]),
                             allow_slow_non_contiguous=True).then_inc(qk_loaded, 16)
            done = R + 1
            load("L1_W", a["L1_gnn_W"], rgcn_done, done + 1)
            load("L2_W1_0", a["L2_gnn_W1"][0], rgcn_done, done + 2)
            load("L2_W1_1", a["L2_gnn_W1"][1], rgcn_done, done + 3)
            load("L2_W1_2", a["L2_gnn_W1"][2], rgcn_done, done + 4)
            load_bias(0, a["L1_gnn_b"], h_ready, 1)
            load_bias(1, a["L2_gnn_b1"], h_ready, 2)
            load("L2_W2_0", a["L2_gnn_W2"][0], hg_done, 2)
            load_bias(2, a["L2_gnn_b2"], hi_ready, 2)
            load("L2_W2_1", a["L2_gnn_W2"][1], alpha_done, 2)
            load("L2_W2_2", a["L2_gnn_W2"][2])
            load_bias(3, a["L3_gnn_b1"], alpha_pre, 2)
            load("L3_W1", a["L3_gnn_W1"], proj_done, 1)
            load_bias(0, a["L3_gnn_b2"], x_ready, 3)
            load("L3_W2", a["L3_gnn_W2"], rel_done, 1)
            sp.wait_ge(x_ready, 6)
            for h in range(2):
                sp.dma_start(out[:, h * HD:(h + 1) * HD], t0[h * N:(h + 1) * N, :]).then_inc(out_stored, 16)
            sp.wait_ge(out_stored, 32)

        @block.gpsimd
        def _(pool):
            made = [0]

            def link(ins):
                made[0] += 1
                ins.then_inc(pool_chain, 1)
                pool.wait_ge(pool_chain, made[0])

            link(nc.gpsimd.iota(cols_i, pattern=[[1, R * N]], base=0, channel_multiplier=0))
            nc.gpsimd.tensor_copy(cols_f, cols_i).then_inc(consts_ready, 1)
            link(nc.gpsimd.memset(ident[:, :], 0.0))
            nc.gpsimd.affine_select(out=ident[:, :], in_=ident[:, :], compare_op=ALU.not_equal, fill=1.0,
                                    base=0, pattern=[[-1, P]], channel_multiplier=1).then_inc(ident_ready, 1)
            pool.wait_ge(ident_ready, 1)
            nc.gpsimd.memset(blockd, 0.0).then_inc(consts_ready, 1)
            nc.gpsimd.tensor_copy(adjT[:, R, :], ident[:, :]).then_inc(consts_ready, 1)
            link(nc.gpsimd.tensor_tensor(avg[:, 0:N], ident[:, 0:N], ident[:, N:P], ALU.add))
            link(nc.gpsimd.tensor_scalar(avg[:, 0:N], avg[:, 0:N], 0.5, None, ALU.mult))
            link(nc.gpsimd.tensor_copy(avg[:, N:P], avg[:, 0:N]))
            link(nc.gpsimd.memset(rsel[:, :], 0.0))
            link(nc.gpsimd.memset(rsel[0:L, N - 1:N], 1.0))
            link(nc.gpsimd.memset(rsel[L:P, N - 1 + NB:N + NB], 1.0))
            link(nc.gpsimd.memset(i3[:, :], 0.0))
            for g in range(3):
                rows = i3[g * GN:(g + 1) * GN, :]
                link(nc.gpsimd.affine_select(out=rows, in_=rows, compare_op=ALU.not_equal, fill=1.0, base=0,
                                             pattern=[[-1, GN]], channel_multiplier=1))
            for g in range(PPG):
                rows = i3[:, g * 2 * NB:(g + 1) * 2 * NB].rearrange("p (b n) -> p n b", b=2)
                nc.gpsimd.tensor_copy(bsel[:, g * NB:(g + 1) * NB, :].rearrange("p n (b l) -> p n b l", b=2),
                                      rows.unsqueeze(3).to_broadcast([3 * GN, NB, 2, L])).then_inc(consts_ready, 1)

            for layer in range(2):
                for t in range(TILES):
                    T = layer * TILES + t
                    if not on_pool(T):
                        continue
                    pool.wait_ge(sig_ready, T + 1)
                    if T >= PRODS:
                        pool.wait_ge(reduced, T - PRODS + 1)
                    nc.gpsimd.tensor_tensor(prod[:, T % PRODS, :], pre[:, T % PRES, :],
                                            qn[:, t // NB, :], ALU.mult).then_inc(prod_p, 1)

        @block.scalar
        def _(act):
            made = [0]

            def link(ins):
                made[0] += 1
                ins.then_inc(act_chain, 1)
                act.wait_ge(act_chain, made[0])

            for g in range(G_QH):
                if group_on_act(g):
                    copy_group(act, g, turned_out_s)
                if g == KC - 1:
                    act.wait_ge(deg_ready, 1)
                    nc.scalar.activation(small[:, 9:10], small[:, 8:9], ACT.Sqrt).then_inc(sqrt_deg, 1)
            def unit_copy(u):
                act.wait_ge(qg_done, u + 1)
                nc.scalar.copy(qg[:, u // 2, HD:D], ps[:, unit_bank(u), 0:HD]).then_inc(qg_out_s, 1)

            for u in range(1, UNITS - 1, 2):
                unit_copy(u)

            def mix_copy(layer):
                act.wait_ge(mixed, 3 * layer + 2)
                nc.scalar.copy(mixT[:, 1, :], ps[:, 1, :]).then_inc(mix_out_s, 1)

            for layer in range(2):
                mix_copy(layer)
                if layer == 0:
                    for k in range(len(EARLY)):
                        copy_group(act, G_QH + k, turned_out_s)
                for i, (part, ready, stacked) in enumerate(((hi, hi_ready, hi_stacked), (mid, mid_ready, mid_stacked))):
                    act.wait_ge(ready, layer + 1)
                    for h in range(2):
                        for g in range(2):
                            nc.scalar.copy(stack[i * GN:(i + 1) * GN, h, g, :],
                                           part[h * N + g * GN:h * N + (g + 1) * GN, :]).then_inc(stacked, 1)
                if layer == 0:
                    unit_copy(UNITS - 1)
                    act.wait_ge(qg_out_s, NP)
                for t in range(TILES):
                    T = layer * TILES + t
                    if layer == 0 and t > 0:
                        for k in range(late_groups(t - 1), late_groups(t)):
                            copy_group(act, G_QH + k, turned_out_s)
                    act.wait_ge(pre_ready, T + 1)
                    src = by_half(pre[:, T % PRES, :])
                    dst = src
                    if not on_pool(T):
                        dst = ps[:, GATE:GATE + 2, 0:HD]
                        if vec_tiles(T):
                            act.wait_ge(prod_v, vec_tiles(T))
                    nc.scalar.activation(dst, src, ACT.Sigmoid).then_inc(sig_ready, 1)
                if layer == 0:
                    for k in range(late_groups(TILES - 1), 2 * GROUPS):
                        copy_group(act, G_QH + k, turned_out_s)
                act.wait_ge(qi_ready, layer + 1)
                nc.scalar.activation(t2[:, :], t0[:, :], ACT.Tanh).then_inc(tanh_ready, 1)
                act.wait_ge(alpha_pre, layer + 1)
                nc.scalar.activation(t1[:, :], t1[:, :], ACT.Sigmoid).then_inc(alpha_ready, 1)

            def ln(n):
                act.wait_ge(ln_var, n)
                nc.scalar.activation(small[:, 5:6], small[:, 4:5], ACT.Sqrt).then_inc(ln_std, 1)

            ln(1)
            ln(2)
            for layer in range(2):
                hp = 2 - layer
                act.wait_ge(rel_done, 2 * layer + 1)
                nc.scalar.copy(X01[:, HD:D], ps[:, 1, 0:HD]).then_inc(X_out_s, 1)
                act.wait_ge(rel_done, 2 * layer + 2)
                nc.scalar.copy(X2[:, HD:D], ps[N:P, 2, 0:HD]).then_inc(X_out_s, 1)
                act.wait_ge(X_turned, 3 * layer + 2)
                nc.scalar.copy(XT[:, JC:KC, 0:P], ps[:, 4, 0:HD].rearrange("p (k n) -> p k n", k=JC)).then_inc(XT_out_s, 1)
                act.wait_ge(shifted, layer + 1)
                n = R * N
                for h in range(hp):
                    nc.scalar.activation(expd[:, h * n:(h + 1) * n], score[:, h * n:(h + 1) * n], ACT.Exp,
                                         bias=small[:, 16 + h:17 + h]).then_inc(exp_ready, 1)
                act.wait_ge(wts_turned, layer + 1)
                nc.scalar.copy(wT2[:, 0:hp * P], ps[0:N, 7, 0:hp * P]).then_inc(wT_out_s, 1)
                if layer == 0:
                    act.wait_ge(elu_min, 1)
                    nc.scalar.activation(t2[:, :], t2[:, :], ACT.Exp).then_inc(elu_exp, 1)
            ln(3)
            ln(4)

        @block.vector
        def _(dve):
            made = [0]

            def link(ins):
                made[0] += 1
                ins.then_inc(vec_chain, 1)
                dve.wait_ge(vec_chain, made[0])

            dve.wait_ge(edges_loaded, 48)
            link(nc.vector.tensor_copy(edge_f, eidx[:, :, :]))
            link(nc.vector.scalar_tensor_tensor(out=edge_f[:, 0, :], in0=edge_f[:, 2, :], scalar=float(N),
                                                in1=edge_f[:, 0, :], op0=ALU.mult, op1=ALU.add))
            dve.wait_ge(consts_ready, 1)
            nc.vector.tensor_tensor(hot_src, cols_f.unsqueeze(1).to_broadcast([P, EC, R * N]),
                                    edge_f[:, 0, :].unsqueeze(2).to_broadcast([P, EC, R * N]),
                                    ALU.is_equal).then_inc(hot_ready, 1)
            for h in range(2):
                nc.vector.tensor_tensor(hot_dst[:, :, h * N:(h + 1) * N], cols_f[:, 0:N].unsqueeze(1).to_broadcast([P, EC, N]),
                                        edge_f[:, 1, :].unsqueeze(2).to_broadcast([P, EC, N]),
                                        ALU.is_equal).then_inc(hot_ready, 1)
            def copy_groups(gs):
                for g in gs:
                    if not group_on_act(g):
                        copy_group(dve, g, turned_out_v)

            dve.wait_ge(counts_done, 1)
            link(nc.vector.tensor_copy(M[:, :], ps[:, 0, 0:R * N]))
            copy_groups(range(KC))
            link(nc.vector.tensor_scalar(maskb[:, :], M[:, :], 0.0, NEG, ALU.is_equal, ALU.mult))
            link(nc.vector.tensor_reduce(small[:, 0:R], M[:, :].rearrange("p (r n) -> p r n", r=R), AX.X, ALU.add))
            link(nc.vector.tensor_reduce(small[:, 7:8], small[:, 0:R], AX.X, ALU.add))
            nc.vector.tensor_scalar(small[:, 8:9], small[:, 7:8], 1.0, None, ALU.add).then_inc(deg_ready, 1)
            link(nc.vector.tensor_scalar(small[:, 0:R], small[:, 0:R], 1.0, None, ALU.max))
            link(nc.vector.reciprocal(small[:, 10:10 + R], small[:, 0:R]))
            copy_groups(range(KC, G_Q))
            dve.wait_ge(consts_ready, 3)
            for h in range(2):
                rows = slice(h * N, (h + 1) * N)
                m3 = M[rows, :].rearrange("p (r n) -> p r n", r=R)
                link(nc.vector.tensor_tensor(blockd[rows, 0:R, rows], m3,
                                             small[rows, 10:10 + R].unsqueeze(2).to_broadcast([N, R, N]), ALU.mult))
                link(nc.vector.tensor_reduce(blockd[rows, R, rows], M[rows, :].rearrange("p (r n) -> p n r", r=R),
                                             AX.X, ALU.add))
            link(nc.vector.tensor_tensor(blockd[:, R, :], blockd[:, R, :], ident[:, :], ALU.add))
            dve.wait_ge(sqrt_deg, 1)
            link(nc.vector.reciprocal(small[:, 13:14], small[:, 9:10]))
            nc.vector.tensor_scalar(blockd[:, R, :], blockd[:, R, :], small[:, 13:14], None, ALU.mult).then_inc(blocks_ready, 1)
            dve.wait_ge(adj_turned, 1)
            nc.vector.tensor_copy(adjT[:, 0:R, :], ps[:, 1, 0:R * P].rearrange("p (r n) -> p r n", r=R)).then_inc(adj_ready, 1)
            nc.vector.tensor_scalar(gcnT[:, :], ps[:, 1, R * P:(R + 1) * P], small[:, 13:14], None, ALU.mult).then_inc(adj_ready, 1)

            copy_groups(range(G_Q, G_QH))
            for u in range(0, UNITS, 2):
                dve.wait_ge(qg_done, u + 1)
                nc.vector.tensor_copy(qg[:, u // 2, 0:HD], ps[:, unit_bank(u), 0:HD]).then_inc(qg_out_v, 1)

            def layer_norm(y, dst, n):
                link(nc.vector.bn_stats(small[:, 20:26], y))
                nc.vector.bn_aggr(small[:, 0:2], small[:, 20:26]).then_inc(ln_parts, 1)
                dve.wait_ge(ln_mean, n)
                dve.wait_ge(ln_parts, n)
                link(nc.vector.tensor_copy(small[:, 2:4], ps[:, TRB, 0:2]))
                link(nc.vector.tensor_tensor(small[:, 6:7], small[:, 0:1], small[:, 2:3], ALU.subtract))
                link(nc.vector.scalar_tensor_tensor(out=small[:, 4:5], in0=small[:, 6:7], scalar=small[:, 6:7],
                                                    in1=small[:, 3:4], op0=ALU.mult, op1=ALU.add))
                nc.vector.tensor_scalar(small[:, 4:5], small[:, 4:5], LN_EPS, None, ALU.add).then_inc(ln_var, 1)
                dve.wait_ge(ln_std, n)
                link(nc.vector.reciprocal(small[:, 6:7], small[:, 5:6]))
                nc.vector.tensor_scalar(dst, y, small[:, 2:3], small[:, 6:7], ALU.subtract, ALU.mult).then_inc(x_ready, 1)

            for layer in range(2):
                for i, j in enumerate((0, 2)):
                    dve.wait_ge(mixed, 3 * layer + j + 1)
                    nc.vector.tensor_copy(mixT[:, j, :], ps[:, j, :]).then_inc(mix_out_v, 1)
                dve.wait_ge(rgcn_done, (R + 1) * (layer + 1))
                dve.wait_ge(bias_loaded[layer], 32)
                link(nc.vector.tensor_tensor(t0[:, :], ps[:, ACC, 0:HD], bias[:, layer, :], ALU.add))
                nc.vector.tensor_scalar(hh[:, :], t0[:, :], 0.0, None, ALU.max).then_inc(h_ready, 1)
                dve.wait_ge(node_turned, layer + 1)
                nc.vector.tensor_copy(nodeT[:, :, :], ps[:, 3, 0:HD].rearrange("p (j n) -> p j n", j=JC)).then_inc(nodeT_ready, 1)
                dve.wait_ge(hg_done, layer + 1)
                dve.wait_ge(bias_loaded[2], 32)
                link(nc.vector.tensor_tensor(t0[:, :], ps[:, 4, 0:HD], bias[:, 2, :], ALU.add))
                nc.vector.tensor_copy(hi[:, :], t0[:, :]).then_inc(hi_ready, 1)
                dve.wait_ge(hi_ready, layer + 1)
                link(nc.vector.tensor_tensor(t1[:, :], t0[:, :], hi[:, :], ALU.subtract))
                nc.vector.tensor_copy(mid[:, :], t1[:, :]).then_inc(mid_ready, 1)
                dve.wait_ge(mid_ready, layer + 1)
                for h in range(2):
                    for g in range(2):
                        r = slice(h * N + g * GN, h * N + (g + 1) * GN)
                        nc.vector.tensor_tensor(stack[2 * GN:3 * GN, h, g, :], t1[r, :], mid[r, :],
                                                ALU.subtract).then_inc(lo_stacked, 1)
                LAG = 2
                for t in range(TILES + LAG):
                    T = layer * TILES + t
                    if t == (NP - 1) * NB:
                        wait_units_out(dve, UNITS)
                    elif t == 0:
                        wait_units_out(dve, UNITS - 1)
                    if t < TILES:
                        dve.wait_ge(hg_cast, T + 1)
                        if T >= PRES:
                            if on_pool(T - PRES):
                                dve.wait_ge(prod_p, pool_tiles(T - PRES + 1))
                            else:
                                dve.wait_ge(sig_ready, T - PRES + 1)
                        nc.vector.tensor_tensor(by_half(pre[:, T % PRES, :]), ring(T), by_half(qg[:, t // NB, :]),
                                                ALU.add).then_inc(pre_ready, 1)
                    if t >= LAG and not on_pool(T - LAG):
                        T -= LAG
                        dve.wait_ge(sig_ready, T + 1)
                        if T >= PRODS:
                            dve.wait_ge(reduced, T - PRODS + 1)
                        nc.vector.tensor_tensor(by_half(prod[:, T % PRODS, :]), ps[:, GATE:GATE + 2, 0:HD],
                                                by_half(qn[:, (t - LAG) // NB, :]), ALU.mult).then_inc(prod_v, 1)
                dve.wait_ge(reduced, (layer + 1) * TILES)
                nc.vector.tensor_copy(t0[:, :], ps[:, ACC, 0:HD]).then_inc(qi_ready, 1)
                dve.wait_ge(qi_turned, layer + 1)
                nc.vector.tensor_copy(qiT[:, :, :], ps[:, 0, 0:HD].rearrange("p (j n) -> p j n", j=JC)).then_inc(qiT_ready, 1)
                dve.wait_ge(tanh_ready, layer + 1)
                link(nc.vector.tensor_tensor(t2[:, :], t2[:, :], hh[:, :], ALU.subtract))
                dve.wait_ge(alpha_done, layer + 1)
                dve.wait_ge(bias_loaded[3], 32)
                nc.vector.tensor_tensor(t1[:, :], ps[:, TRB, 0:HD], bias[:, 3, :], ALU.add).then_inc(alpha_pre, 1)
                dve.wait_ge(alpha_ready, layer + 1)
                link(nc.vector.tensor_tensor(t1[:, :], t1[:, :], t2[:, :], ALU.mult))
                ins = nc.vector.tensor_tensor(hx[:, :], t1[:, :], hh[:, :], ALU.add)
                if layer == 0:
                    ins.then_inc(x_ready, 1)
                else:
                    link(ins)
            link(nc.vector.tensor_tensor(t0[:, :], hx[:, :], xa[:, :], ALU.add))
            layer_norm(t0[:, :], xa[:, :], 1)

            def gcn_mix(n):
                dve.wait_ge(node_turned, n)
                nc.vector.tensor_copy(nodeT[:, :, :], ps[:, 3, 0:HD].rearrange("p (j n) -> p j n", j=JC)).then_inc(nodeT_ready, 1)

            gcn_mix(3)
            dve.wait_ge(proj_done, 1)
            dve.wait_ge(bias_loaded[0], 64)
            link(nc.vector.tensor_tensor(t0[:, :], ps[:, ACC, 0:HD], bias[:, 0, :], ALU.add))
            link(nc.vector.tensor_tensor(t0[:, :], t0[:, :], xa[:, :], ALU.add))
            layer_norm(t0[:, :], xa[:, :], 2)

            for layer in range(2):
                hp = 2 - layer
                bw = HD // hp
                n = R * N
                gcn_mix(4 + layer)
                dve.wait_ge(rel_done, 2 * layer + 1)
                nc.vector.tensor_copy(X01[:, 0:HD], ps[:, 0, 0:HD]).then_inc(X_out_v, 1)
                dve.wait_ge(rel_done, 2 * layer + 2)
                nc.vector.tensor_copy(X2[:, 0:HD], ps[0:N, 2, 0:HD]).then_inc(X_out_v, 1)
                dve.wait_ge(X_turned, 3 * layer + 1)
                nc.vector.tensor_copy(XT[:, 0:JC, 0:P], ps[:, 3, 0:HD].rearrange("p (k n) -> p k n", k=JC)).then_inc(XT_out_v, 1)
                dve.wait_ge(X_turned, 3 * layer + 3)
                nc.vector.tensor_copy(XT[:, :, P:n], ps[:, 5, 0:HD].rearrange("p (k n) -> p k n", k=KC)).then_inc(XT_out_v, 1)
                dve.wait_ge(qk_done, layer + 1)
                nc.vector.tensor_copy(QKT[0:4 * hp if hp == 2 else 2, :], ps[0:4 * hp if hp == 2 else 2, 6, 0:n]).then_inc(qkT_ready, 1)
                dve.wait_ge(score_done, layer + 1)
                link(nc.vector.tensor_copy(small[:, 26:26 + R * hp], ps[:, 1, 0:R * hp]))
                sc4 = score[:, 0:hp * n].rearrange("p (h r n) -> p h r n", h=hp, r=R)
                qv = small[:, 26:26 + R * hp].rearrange("p (r h) -> p h r", h=hp)
                link(nc.vector.tensor_tensor(sc4, ps[:, 0, 0:hp * n].rearrange("p (h r n) -> p h r n", h=hp, r=R),
                                             qv.unsqueeze(3).to_broadcast([P, hp, R, N]), ALU.add))
                link(nc.vector.scalar_tensor_tensor(out=leaky[:, 0:hp * n], in0=score[:, 0:hp * n], scalar=SLOPE,
                                                    in1=score[:, 0:hp * n], op0=ALU.mult, op1=ALU.max))
                sc3 = score[:, 0:hp * n].rearrange("p (h c) -> p h c", h=hp)
                link(nc.vector.tensor_tensor(sc3, leaky[:, 0:hp * n].rearrange("p (h c) -> p h c", h=hp),
                                             maskb[:, :].unsqueeze(1).to_broadcast([P, hp, n]), ALU.add))
                nc.vector.tensor_reduce(small[:, 16:16 + hp], sc3, AX.X, ALU.max, negate=True).then_inc(shifted, 1)
                for h in range(hp):
                    dve.wait_ge(exp_ready, 2 * layer + h + 1)
                    nc.vector.tensor_tensor_reduce(wts[:, h * n:(h + 1) * n], expd[:, h * n:(h + 1) * n], M[:, :], 1.0, 0.0,
                                                   ALU.mult, ALU.add, small[:, 18 + h:19 + h]).then_inc(wts_ready, 1)
                dve.wait_ge(wts_turned, layer + 1)
                nc.vector.tensor_copy(wT1[:, 0:hp * P], ps[:, 3, 0:hp * P]).then_inc(wT_out_v, 1)
                link(nc.vector.tensor_scalar(small[:, 18:18 + hp], small[:, 18:18 + hp], SOFTMAX_EPS, None, ALU.add))
                link(nc.vector.reciprocal(small[:, 32:32 + hp], small[:, 18:18 + hp]))
                dve.wait_ge(att_done, layer + 1)
                dve.wait_ge(bias_loaded[1 + layer], 64)
                for h in range(hp):
                    ins = nc.vector.scalar_tensor_tensor(out=t0[:, h * bw:(h + 1) * bw], in0=ps[:, ACC, h * bw:(h + 1) * bw],
                                                         scalar=small[:, 32 + h:33 + h], in1=bias[:, 1 + layer, h * bw:(h + 1) * bw],
                                                         op0=ALU.mult, op1=ALU.add)
                    link(ins)
                if layer == 0:
                    nc.vector.tensor_scalar(t2[:, :], t0[:, :], 0.0, None, ALU.min).then_inc(elu_min, 1)
                    link(nc.vector.tensor_scalar(t0[:, :], t0[:, :], 0.0, None, ALU.max))
                    dve.wait_ge(elu_exp, 1)
                    nc.vector.scalar_tensor_tensor(out=hx[:, :], in0=t2[:, :], scalar=-1.0, in1=t0[:, :],
                                                   op0=ALU.add, op1=ALU.add).then_inc(x_ready, 1)
                else:
                    link(nc.vector.tensor_tensor(t0[:, :], t0[:, :], xa[:, :], ALU.add))
                    layer_norm(t0[:, :], xa[:, :], 3)
            gcn_mix(6)
            dve.wait_ge(proj_done, 2)
            dve.wait_ge(bias_loaded[3], 64)
            link(nc.vector.tensor_tensor(t0[:, :], ps[:, ACC, 0:HD], bias[:, 3, :], ALU.add))
            nc.vector.tensor_scalar(hx[:, :], t0[:, :], 0.0, None, ALU.max).then_inc(y_ready, 1)
            gcn_mix(7)
            dve.wait_ge(proj_done, 3)
            dve.wait_ge(bias_loaded[0], 96)
            link(nc.vector.tensor_tensor(t1[:, :], ps[:, ACC, 0:HD], bias[:, 0, :], ALU.add))
            link(nc.vector.tensor_tensor(t1[:, :], t1[:, :], xa[:, :], ALU.add))
            layer_norm(t1[:, :], t0[:, :], 4)

        @block.tensor
        def _(pe):
            def turn_blocks(g, blocks):
                at = 0
                for src in blocks:
                    ins = nc.tensor.transpose(ps[:, group_bank(g), at:at + P], src, ident[:, :])
                    at += P
                ins.then_inc(turned, 1)

            def turn_weight(g0, key, k):
                part, col = k // KC, k % KC
                if col == 0:
                    wait_loaded(pe, key, part)
                if g0 < G_QH:
                    if g0 + k >= 4:
                        wait_group_out(pe, g0 + k - 4)
                elif g0 + k >= G_QH + len(EARLY):
                    wait_group_out(pe, g0 + k - 1)
                src = W[SLOT[key]]
                turn_blocks(g0 + k, [src[:, part * JC + i, col * P:(col + 1) * P] for i in range(JC)])

            def project(T, w, bank, first=True, last=True, col0=0):
                for k in range(KC):
                    h, j = k // JC, k % JC
                    for c in range(2):
                        ins = nc.tensor.matmul(ps[c * N:(c + 1) * N, bank, 0:HD],
                                               T[:, j, col0 + h * N:col0 + (h + 1) * N],
                                               w[:, k, c * HD:(c + 1) * HD],
                                               start=(first and k == 0), stop=(last and k == KC - 1),
                                               skip_group_check=True)
                return ins

            def turn_nodes(y, bank, right):
                for j in range(JC):
                    out_j = ps[:, bank, j * P:(j + 1) * P]
                    if right is ident:
                        ins = nc.tensor.transpose(out_j, y[:, j * P:(j + 1) * P], ident[:, :])
                    else:
                        ins = nc.tensor.matmul(out_j, y[:, j * P:(j + 1) * P], right[:, :], start=True, stop=True)
                return ins

            pe.wait_ge(hot_ready, 3)
            for c in range(EC):
                ins = nc.tensor.matmul(ps[:, 0, 0:R * N], hot_dst[:, c, :], hot_src[:, c, :],
                                       start=(c == 0), stop=(c == EC - 1))
            ins.then_inc(counts_done, 1)
            pe.wait_ge(ident_ready, 1)
            for k in range(GROUPS):
                turn_weight(0, "Wg_q", k)
            pe.wait_ge(blocks_ready, 1)
            for r in range(R + 1):
                ins = nc.tensor.transpose(ps[:, 1, r * P:(r + 1) * P], blockd[:, r, :], ident[:, :])
            ins.then_inc(adj_turned, 1)
            pe.wait_ge(q_loaded, 32)
            for k in range(NQG):
                wait_group_out(pe, G_Q + k - 4)
                turn_blocks(G_Q + k, [qn[:, p, k * P:(k + 1) * P] for p in range(NP)])
            for k in range(GROUPS):
                turn_weight(G_H, "Wg_h", k)
            wait_groups_out(pe, G_H)
            pe.wait_ge(adj_ready, 2)
            def query_unit(u):
                if 4 <= u < UNITS - 1:
                    wait_units_out(pe, u - 3)
                p, c = u // 2, u % 2
                for k in range(KC):
                    ins = nc.tensor.matmul(ps[:, unit_bank(u), 0:HD], qT[:, k, p * P:(p + 1) * P],
                                           WgT_q[:, k, c * HD:(c + 1) * HD], start=(k == 0), stop=(k == KC - 1))
                ins.then_inc(qg_done, 1)

            def turn_wq(ks):
                for k in ks:
                    turn_weight(G_QH + (k // GROUPS) * GROUPS, ("Wq_h", "Wq_q")[k // GROUPS], k % GROUPS)

            for u in range(UNITS - 1):
                query_unit(u)

            def gate(layer):
                if layer == 0:
                    pe.wait_ge(consts_ready, 5)
                LAG = 5
                for t in range(TILES + LAG):
                    T = layer * TILES + t
                    if t == 0:
                        pe.wait_ge(hi_stacked, 4 * (layer + 1))
                        pe.wait_ge(mid_stacked, 4 * (layer + 1))
                        pe.wait_ge(lo_stacked, 4 * (layer + 1))
                    if t < TILES:
                        if T >= RING:
                            pe.wait_ge(pre_ready, T - RING + 1)
                        p, n = t // NB, t % NB
                        for c in range(2):
                            ins = nc.tensor.matmul(ring(T)[:, c, :], bsel[:, (p % PPG) * NB + n, :],
                                                   stack[:, c, p // PPG, :], start=True, stop=True)
                        ins.then_inc(hg_cast, 1)
                    if layer == 0 and t < TILES:
                        turn_wq(range(late_groups(t), late_groups(t + 1)))
                    if t == TILES:
                        if layer == 0:
                            wait_groups_out(pe, G_END)
                        project(nodeT, WqT_h, TRB, last=False)
                    if t >= LAG:
                        T -= LAG
                        if on_pool(T):
                            pe.wait_ge(prod_p, pool_tiles(T + 1))
                        else:
                            pe.wait_ge(prod_v, vec_tiles(T + 1))
                        s = N - 1 - (2 * NB * ((t - LAG) // NB) + (t - LAG) % NB)
                        for c in range(2):
                            ins = nc.tensor.matmul(ps[c * N:(c + 1) * N, ACC, 0:HD], rsel[:, s:s + N],
                                                   prod[:, T % PRODS, c * HD:(c + 1) * HD],
                                                   start=(t == LAG), stop=(t == TILES + LAG - 1), skip_group_check=True)
                        ins.then_inc(reduced, 1)

            for layer in range(2):
                x = xa if layer == 0 else hx
                if layer == 0:
                    pe.wait_ge(x_loaded, 32)
                    wait_units_out(pe, UNITS - 1)
                    wait_groups_out(pe, G_QH)
                else:
                    pe.wait_ge(x_ready, 1)
                for j in range(JC):
                    nc.tensor.matmul(ps[:, j, :], x[:, j * P:(j + 1) * P], adjT[:, :, :].rearrange("p r n -> p (r n)"),
                                     start=True, stop=True).then_inc(mixed, 1)
                pe.wait_ge(mix_out_v, 2 * (layer + 1))
                pe.wait_ge(mix_out_s, layer + 1)
                for r in range(R + 1):
                    key = f"rel{layer + 1}_{r}" if r < R else f"root{layer + 1}"
                    wait_loaded(pe, key)
                    project(mixT, W[SLOT[key]], ACC, first=(r == 0), last=(r == R),
                            col0=r * P).then_inc(rgcn_done, 1)
                if layer == 0:
                    turn_wq(range(0, 3))
                pe.wait_ge(h_ready, layer + 1)
                turn_nodes(hh, 3, ident).then_inc(node_turned, 1)
                if layer == 0:
                    turn_wq(range(3, len(EARLY)))
                pe.wait_ge(nodeT_ready, layer + 1)
                project(nodeT, WgT_h, 4).then_inc(hg_done, 1)
                if layer == 0:
                    wait_groups_out(pe, G_QH + len(EARLY))
                    query_unit(UNITS - 1)
                gate(layer)
                pe.wait_ge(qi_ready, layer + 1)
                turn_nodes(t0, 0, ident).then_inc(qi_turned, 1)
                pe.wait_ge(qiT_ready, layer + 1)
                project(qiT, WqT_q, TRB, first=False).then_inc(alpha_done, 1)

            def norm_stats(n):
                pe.wait_ge(ln_parts, n)
                nc.tensor.matmul(ps[:, TRB, 0:2], avg[:, :], small[:, 0:2], start=True, stop=True).then_inc(ln_mean, 1)

            def gcn(n, key, x, bank=ACC):
                turn_nodes(x, 3, gcnT).then_inc(node_turned, 1)
                pe.wait_ge(nodeT_ready, n)
                wait_loaded(pe, key)
                project(nodeT, W[SLOT[key]], bank).then_inc(proj_done, 1)

            norm_stats(1)
            pe.wait_ge(x_ready, 2)
            gcn(3, "L1_W", xa)
            norm_stats(2)

            pe.wait_ge(qk_loaded, 64)
            for layer in range(2):
                hp = 2 - layer
                bw = HD // hp
                m = 4 * hp if hp == 2 else 2
                n = R * N
                x = xa if layer == 0 else hx
                pe.wait_ge(x_ready, 3 + layer)
                turn_nodes(x, 3, ident).then_inc(node_turned, 1)
                pe.wait_ge(nodeT_ready, 4 + layer)
                keys = [f"L2_W{layer + 1}_{r}" for r in range(R)]
                wait_loaded(pe, keys[0])
                wait_loaded(pe, keys[1])
                for k in range(KC):
                    h, j = k // JC, k % JC
                    for c in range(2):
                        for r in range(2):
                            ins = nc.tensor.matmul(ps[r * N:(r + 1) * N, c, 0:HD], nodeT[:, j, h * N:(h + 1) * N],
                                                   W[SLOT[keys[r]]][:, k, c * HD:(c + 1) * HD],
                                                   start=(k == 0), stop=(k == KC - 1), skip_group_check=True)
                ins.then_inc(rel_done, 1)
                wait_loaded(pe, keys[2])
                project(nodeT, W[SLOT[keys[2]]], 2).then_inc(rel_done, 1)
                for part in range(2):
                    pe.wait_ge((X_out_v, X_out_s)[part], 2 * layer + 1)
                    for i in range(JC):
                        k = part * JC + i
                        ins = nc.tensor.transpose(ps[:, 3 + part, i * P:(i + 1) * P], X01[:, k * P:(k + 1) * P], ident[:, :])
                    ins.then_inc(X_turned, 1)
                pe.wait_ge(X_out_v, 2 * layer + 2)
                pe.wait_ge(X_out_s, 2 * layer + 2)
                for k in range(KC):
                    ins = nc.tensor.transpose(ps[:, 5, k * N:(k + 1) * N], X2[:, k * P:(k + 1) * P], ident[0:N, 0:N])
                ins.then_inc(X_turned, 1)
                pe.wait_ge(XT_out_v, 2 * layer + 2)
                pe.wait_ge(XT_out_s, layer + 1)
                for k in range(KC):
                    ins = nc.tensor.matmul(ps[0:m, ACC, 0:n], (qk, qk2)[layer][:, k, 0:m], XT[:, k, :],
                                           start=(k == 0), stop=(k == KC - 1))
                ins.then_inc(qk_done, 1)
                pe.wait_ge(qkT_ready, layer + 1)
                for h in range(hp):
                    for half in range(2):
                        row = m // 2 + (hp * half + h if hp == 2 else 0)
                        nc.tensor.matmul(ps[half * N:(half + 1) * N, 0, h * n:(h + 1) * n],
                                         ident[0:m, row:row + 1].to_broadcast([m, N]), QKT[0:m, :],
                                         start=True, stop=True, skip_group_check=True)
                for r in range(R):
                    for half in range(2):
                        row = hp * half if hp == 2 else 0
                        ins = nc.tensor.matmul(ps[half * N:(half + 1) * N, 1, r * hp:(r + 1) * hp],
                                               QKT[0:m, r * N:(r + 1) * N], ident[0:m, row:row + hp],
                                               start=True, stop=True, skip_group_check=True)
                ins.then_inc(score_done, 1)
                pe.wait_ge(wts_ready, 2 * layer + hp)
                for h in range(hp):
                    nc.tensor.transpose(ps[:, 3, h * P:(h + 1) * P], wts[:, h * n:h * n + P], ident[:, :])
                for h in range(hp):
                    ins = nc.tensor.transpose(ps[0:N, 7, h * P:(h + 1) * P], wts[:, h * n + P:(h + 1) * n], ident[:, :])
                ins.then_inc(wts_turned, 1)
                pe.wait_ge(wT_out_v, layer + 1)
                pe.wait_ge(wT_out_s, layer + 1)
                for h in range(hp):
                    for half in range(2):
                        at = half * HD + h * bw
                        nc.tensor.matmul(ps[half * N:(half + 1) * N, ACC, h * bw:(h + 1) * bw],
                                         wT1[:, h * P + half * N:h * P + (half + 1) * N], X01[:, at:at + bw],
                                         start=True, stop=False, skip_group_check=True)
                        ins = nc.tensor.matmul(ps[half * N:(half + 1) * N, ACC, h * bw:(h + 1) * bw],
                                               wT2[:, h * P + half * N:h * P + (half + 1) * N], X2[:, at:at + bw],
                                               start=False, stop=True, skip_group_check=True)
                ins.then_inc(att_done, 1)
            norm_stats(3)
            pe.wait_ge(x_ready, 5)
            gcn(6, "L3_W1", xa)
            pe.wait_ge(y_ready, 1)
            gcn(7, "L3_W2", hx)
            norm_stats(4)


def kernel(**inputs):
    import numpy as _np
    import concourse.bacc as _bacc
    from concourse import mybir as _mybir
    from concourse.bass_utils import run_bass_kernel_spmd as _run

    nc = _bacc.Bacc("TRN2", target_bir_lowering=False, num_devices=1)
    arrays, aps = {}, {}
    for name, value in inputs.items():
        v = _np.ascontiguousarray(value)
        arrays[f"in_{name}"] = v
        aps[name] = nc.dram_tensor(f"in_{name}", v.shape, _mybir.dt.from_np(v.dtype), kind="ExternalInput").ap()
    shape = arrays["in_x"].shape
    out = nc.dram_tensor("out", shape, _mybir.dt.float32, kind="ExternalOutput").ap()
    gnn_kernel(nc, aps, out)
    r = _run(nc, [arrays], core_ids=[0])
    return r.results[0]["out"]
```

```python
from contextlib import ExitStack

import concourse.bass as bass
from concourse import mybir

ALU = mybir.AluOpType
ACT = mybir.ActivationFunctionType
AX = mybir.AxisListType
F32 = mybir.dt.float32
BF16 = mybir.dt.bfloat16
I32 = mybir.dt.int32

P = 128
NEG = -1.0e30
LN_EPS = 1e-5
SOFTMAX_EPS = 1e-16
SLOPE = 0.2


def gnn_kernel(nc: bass.Bass, a, out):
    N, D = a["x"].shape
    E = a["src"].shape[0]
    R = a["L0_gnn_W_rel1"].shape[0]
    B, L, _ = a["L0_gnn_query_embs"].shape
    NB = N // B
    HD = D // 2
    KC = D // P
    JC = KC // 2
    EC = E // P
    NP = B // 2
    TILES = NP * NB
    GN = 32
    PPG = GN // (2 * NB)
    assert N == 64 and 2 * L == P and 2 * HD == D and KC % 2 == 0


    PLAN = [("Wg_q", 0, 2), ("Wg_h", 3, 2), ("rel1_0", 5, 1), ("rel1_1", 6, 1), ("rel1_2", 0, 1), ("root1", 3, 1),
            ("Wq_h", 5, 2), ("Wq_q", 6, 2), ("rel2_0", 3, 1), ("rel2_1", 2, 1), ("rel2_2", 5, 1), ("root2", 6, 1),
            ("L1_W", 3, 1), ("L2_W1_0", 2, 1), ("L2_W1_1", 5, 1), ("L2_W1_2", 6, 1),
            ("L2_W2_0", 4, 1), ("L2_W2_1", 0, 1), ("L2_W2_2", 1, 1), ("L3_W1", 3, 1), ("L3_W2", 2, 1)]
    SLOT = {key: s for key, s, _ in PLAN}
    PARTS = {key: n for key, _, n in PLAN}

    with ExitStack() as ctx:
        def sb(name, shape, dt=F32):
            return ctx.enter_context(nc.sbuf_tensor(name, shape, dt))

        def sem(name):
            return ctx.enter_context(nc.semaphore(name))

        NSLOT = 7
        W = [sb(f"W{s}", [P, KC, D]) for s in range(NSLOT)]
        qn = sb("qn", [P, NP, D])
        qg = sb("qg", [P, NP, D])
        PRODS = 4
        prod = sb("prod", [P, PRODS, D])
        PRES = 4
        pre = sb("pre", [P, PRES, D])
        BIASES = ["L0_gnn_b1", "L0_gnn_b2", "L0_gnn_bg", "L0_gnn_bq", "L1_gnn_b", "L2_gnn_b1", "L2_gnn_b2",
                  "L3_gnn_b1", "L3_gnn_b2"]
        bias = sb("bias", [len(BIASES), D])
        bias_mid = sb("bias_mid", [len(BIASES), D], BF16)
        biases = sb("biases", [3 * GN, D], BF16)
        nodeT = sb("nodeT", [P, JC, P])
        adjT = sb("adjT", [P, R + 1, P])
        gcnT = sb("gcnT", [P, P])
        ident = sb("ident", [P, P])
        avg = sb("avg", [P, P])
        bsel = sb("bsel", [3 * GN, PPG * NB, P], BF16)
        i3 = sb("i3", [3 * GN, GN], BF16)
        rsel = sb("rsel", [P, P])
        stack = sb("stack", [3 * GN, 2, 2, HD], BF16)
        xa = sb("xa", [P, HD])
        hh = sb("hh", [P, HD])
        hx = sb("hx", [P, HD])
        t0 = sb("t0", [P, HD])
        t1 = sb("t1", [P, HD])
        t2 = sb("t2", [P, HD])
        hi = sb("hi", [P, HD], BF16)
        mid = sb("mid", [P, HD], BF16)
        M = sb("M", [P, R * N])
        maskb = sb("maskb", [P, R * N])
        small = sb("small", [P, 64])
        eidx = sb("eidx", [P, 3, EC], I32)
        qk = sb("qk", [P, KC, 8])
        qk2 = sb("qk2", [P, KC, 2])

        prod_f = prod[:, :, :].rearrange("p a b -> p (a b)")
        hot_src = prod_f[:, 0:EC * R * N // 2].bitcast(BF16).rearrange("p (c k) -> p c k", c=EC)
        o = EC * R * N // 2
        hot_dst = prod_f[:, o:o + EC * P // 2].bitcast(BF16).rearrange("p (c k) -> p c k", c=EC)
        o += EC * P // 2
        blockd = prod_f[:, o:o + (R + 1) * P].rearrange("p (r k) -> p r k", r=R + 1)
        mixT = prod_f[:, 0:JC * (R + 1) * P].rearrange("p (j n) -> p j n", j=JC)
        qiT = prod_f[:, JC * (R + 1) * P:JC * (R + 2) * P].rearrange("p (j n) -> p j n", j=JC)
        pre_f = pre[:, :, :].rearrange("p a b -> p (a b)")
        cols_i = pre_f[:, 0:R * N].bitcast(I32)
        cols_f = pre_f[:, R * N:2 * R * N]
        edge_f = pre_f[:, 2 * R * N:2 * R * N + 3 * EC].rearrange("p (a c) -> p a c", a=3)
        qT = W[2][:, :, 0:NP * P]
        qn_f = qn[:, :, :].rearrange("p a b -> p (a b)")
        qg_f = qg[:, :, :].rearrange("p a b -> p (a b)")
        X01 = qn_f[:, 0:D]
        X2 = qn_f[0:N, D:2 * D]
        XT = qn_f[:, 2 * D:2 * D + KC * R * N].rearrange("p (k n) -> p k n", k=KC)
        score = qg_f[:, 0:HD]
        leaky = qg_f[:, HD:2 * HD]
        expd = qg_f[:, 2 * HD:3 * HD]
        wts = qg_f[:, 3 * HD:4 * HD]
        wT1 = qg_f[:, 4 * HD:4 * HD + 2 * P]
        wT2 = qg_f[0:N, 4 * HD + 2 * P:4 * HD + 4 * P]
        QKT = qg_f[0:8, 6 * HD:6 * HD + R * N]

        ps = ctx.enter_context(nc.psum_tensor("ps", [P, 8, 512], F32))
        RING = 2
        GATE, ACC, TRB = 4, 6, 7
        HG = 4
        ADDEND = 5
        LAST = 5

        def ring(t):
            s = 2 * (t % RING)
            return ps[:, s:s + 2, 0:HD]

        def by_half(tile):
            return tile.rearrange("p (h f) -> p h f", h=2)

        loaded = {key: [sem(f"{key}_{c}_loaded") for c in range(n)] for key, _, n in PLAN}
        edges_loaded = sem("edges_loaded")
        x_loaded = sem("x_loaded")
        q_loaded = sem("q_loaded")
        qk_loaded = sem("qk_loaded")
        bias_loaded = sem("bias_loaded")
        out_stored = sem("out_stored")
        pool_chain = sem("pool_chain")
        vec_chain = sem("vec_chain")
        act_chain = sem("act_chain")
        ident_ready = sem("ident_ready")
        consts_ready = sem("consts_ready")
        hot_ready = sem("hot_ready")
        counts_done = sem("counts_done")
        blocks_ready = sem("blocks_ready")
        adj_turned = sem("adj_turned")
        adj_ready = sem("adj_ready")
        deg_ready = sem("deg_ready")
        sqrt_deg = sem("sqrt_deg")
        turned = sem("turned")
        turned_out_v = sem("turned_out_v")
        turned_out_s = sem("turned_out_s")
        qg_done = sem("qg_done")
        qg_out_v = sem("qg_out_v")
        qg_out_s = sem("qg_out_s")
        mixed = sem("mixed")
        mix_out_v = sem("mix_out_v")
        mix_out_s = sem("mix_out_s")
        rgcn_done = sem("rgcn_done")
        h_ready = sem("h_ready")
        node_turned = sem("node_turned")
        nodeT_ready = sem("nodeT_ready")
        hg_done = sem("hg_done")
        hi_ready = sem("hi_ready")
        mid_ready = sem("mid_ready")
        hi_stacked = sem("hi_stacked")
        mid_stacked = sem("mid_stacked")
        lo_stacked = sem("lo_stacked")
        hg_cast = sem("hg_cast")
        pre_ready = sem("pre_ready")
        sig_ready = sem("sig_ready")
        prod_v = sem("prod_v")
        prod_p = sem("prod_p")
        reduced = sem("reduced")
        qi_ready = sem("qi_ready")
        tanh_ready = sem("tanh_ready")
        qi_turned = sem("qi_turned")
        qiT_ready = sem("qiT_ready")
        alpha_done = sem("alpha_done")
        alpha_ready = sem("alpha_ready")
        x_ready = sem("x_ready")
        ln_parts = sem("ln_parts")
        ln_mean = sem("ln_mean")
        ln_var = sem("ln_var")
        ln_std = sem("ln_std")
        proj_done = sem("proj_done")
        rel_done = sem("rel_done")
        X_out_v = sem("X_out_v")
        X_out_s = sem("X_out_s")
        X_turned = sem("X_turned")
        XT_out_v = sem("XT_out_v")
        XT_out_s = sem("XT_out_s")
        qk_done = sem("qk_done")
        qkT_ready = sem("qkT_ready")
        score_done = sem("score_done")
        shifted = sem("shifted")
        exp_ready = sem("exp_ready")
        wts_ready = sem("wts_ready")
        wts_turned = sem("wts_turned")
        wT_out_v = sem("wT_out_v")
        wT_out_s = sem("wT_out_s")
        biases_split = sem("biases_split")
        addend_done = sem("addend_done")
        att_done = sem("att_done")
        elu_min = sem("elu_min")
        elu_exp = sem("elu_exp")
        y_ready = sem("y_ready")

        POOL_NODES = (0, 2, 3, 5, 6)

        def on_pool(T):
            return T % NB in POOL_NODES

        def pool_tiles(T):
            return sum(on_pool(k) for k in range(T))

        def vec_tiles(T):
            return T - pool_tiles(T)

        GROUPS = 2 * KC

        def group_on_act(g):
            return g >= G_QH or g % 2 == 0

        G_Q = GROUPS
        NQG = KC
        G_H = G_Q + NQG
        G_QH = G_H + GROUPS
        G_END = G_QH + 2 * GROUPS

        def act_groups(g):
            return sum(group_on_act(k) for k in range(g))

        def vec_groups(g):
            return g - act_groups(g)

        def wait_group_out(eng, g):
            if group_on_act(g):
                eng.wait_ge(turned_out_s, act_groups(g + 1))
            else:
                eng.wait_ge(turned_out_v, vec_groups(g + 1))

        def wait_groups_out(eng, g):
            if act_groups(g):
                eng.wait_ge(turned_out_s, act_groups(g))
            if vec_groups(g):
                eng.wait_ge(turned_out_v, vec_groups(g))

        EARLY = (0, 1, 2, 5, 6, 7)
        LATE = 2 * GROUPS - len(EARLY)
        LATE_TILES = 3 * TILES // 4
        ALPHA_AT = [{TILES - KC + k: k for k in range(KC)}, {12 + 3 * k: k for k in range(KC)}]

        def late_groups(t):
            return len(EARLY) + min(t, LATE_TILES) * LATE // LATE_TILES

        def group_bank(g):
            if g < G_QH:
                return 4 + g % 4
            return EARLY[g - G_QH] if g - G_QH < len(EARLY) else TRB

        UNITS = 2 * NP

        def mix_bank(layer, j):
            return j + (5 if layer == 0 else 0)

        def unit_bank(u):
            return u % 4 if u < UNITS - 1 else GATE + 1

        def wait_units_out(eng, u):
            eng.wait_ge(qg_out_v, (u + 1) // 2)
            eng.wait_ge(qg_out_s, u // 2)

        WgT_q, WgT_h, WqT_h, WqT_q = W[1], W[4], W[0], W[1]

        def group_dst(g):
            if g < G_Q:
                return WgT_q[:, g % KC, (g // KC) * HD:(g // KC + 1) * HD], HD
            if g < G_H:
                return qT[:, g - G_Q, :], NP * P
            if g < G_QH:
                k = g - G_H
                return WgT_h[:, k % KC, (k // KC) * HD:(k // KC + 1) * HD], HD
            k = (g - G_QH) % GROUPS
            dst = WqT_h if g - G_QH < GROUPS else WqT_q
            return dst[:, k % KC, (k // KC) * HD:(k // KC + 1) * HD], HD

        def copy_group(eng, g, done):
            dst, n = group_dst(g)
            eng.wait_ge(turned, g + 1)
            src = ps[:, group_bank(g), 0:n]
            ins = nc.vector.tensor_copy(dst, src) if done is turned_out_v else nc.scalar.copy(dst, src)
            ins.then_inc(done, 1)

        def wait_loaded(eng, key, part=0):
            eng.wait_ge(loaded[key][part], 16)

        def halves(dram):
            return dram.rearrange("(k p) n -> p k n", p=P)

        block = ctx.enter_context(nc.Block())

        @block.sync
        def _(sp):
            def load(key, dram, after=None, value=0):
                if after is not None:
                    sp.wait_ge(after, value)
                s = SLOT[key]
                n = KC // PARTS[key]
                v = halves(dram)
                for c in range(PARTS[key]):
                    sp.dma_start(W[s][:, c * n:(c + 1) * n, :], v[:, c * n:(c + 1) * n, :]).then_inc(loaded[key][c], 16)

            for i, name in enumerate(("src", "dst", "edge_type_3")):
                sp.dma_start(eidx[:, i, :], a[name].rearrange("(p c) -> p c", p=P)).then_inc(edges_loaded, 16)
            Wg, Wq = a["L0_gnn_Wg"], a["L0_gnn_Wq"]
            load("Wg_q", Wg[:, D:2 * D])
            for b in range(2):
                sp.dma_start(qn[b * L:(b + 1) * L, :, :],
                             a["L0_gnn_query_embs"].rearrange("(p b) l f -> b l p f", b=2)[b]).then_inc(q_loaded, 16)
            load("Wg_h", Wg[:, 0:D])
            for h in range(2):
                sp.dma_start(xa[h * N:(h + 1) * N, :], a["x"][:, h * HD:(h + 1) * HD]).then_inc(x_loaded, 16)
            load("rel1_0", a["L0_gnn_W_rel1"][0])
            load("rel1_1", a["L0_gnn_W_rel1"][1])
            for i, name in enumerate(BIASES):
                sp.dma_start(bias[i:i + 1, :], a[name].rearrange("(o f) -> o f", o=1)).then_inc(bias_loaded, 16)
            load("rel1_2", a["L0_gnn_W_rel1"][2], turned, GROUPS)
            load("root1", a["L0_gnn_W_root1"], turned, G_QH)
            load("Wq_h", Wq[:, 0:D], rgcn_done, 1)
            load("Wq_q", Wq[:, D:2 * D], rgcn_done, 2)
            load("rel2_0", a["L0_gnn_W_rel2"][0], rgcn_done, R + 1)
            load("rel2_1", a["L0_gnn_W_rel2"][1], qg_done, UNITS)
            load("rel2_2", a["L0_gnn_W_rel2"][2], turned, G_QH + GROUPS)
            load("root2", a["L0_gnn_W_root2"], turned, G_END)
            for q, name in enumerate(("q", "k")):
                sp.dma_start(qk[:, :, 4 * q:4 * q + 4], halves(a[f"L2_gnn_{name}1"]),
                             allow_slow_non_contiguous=True).then_inc(qk_loaded, 16)
                sp.dma_start(qk2[:, :, q:q + 1], halves(a[f"L2_gnn_{name}2"]),
                             allow_slow_non_contiguous=True).then_inc(qk_loaded, 16)
            done = R + 1
            load("L1_W", a["L1_gnn_W"], rgcn_done, done + 1)
            load("L2_W1_0", a["L2_gnn_W1"][0], rgcn_done, done + 2)
            load("L2_W1_1", a["L2_gnn_W1"][1], rgcn_done, done + 3)
            load("L2_W1_2", a["L2_gnn_W1"][2], rgcn_done, done + 4)
            load("L2_W2_0", a["L2_gnn_W2"][0], hg_done, 2)
            load("L2_W2_1", a["L2_gnn_W2"][1], alpha_done, 2)
            load("L2_W2_2", a["L2_gnn_W2"][2])
            load("L3_W1", a["L3_gnn_W1"], proj_done, 1)
            load("L3_W2", a["L3_gnn_W2"], rel_done, 2)
            sp.wait_ge(x_ready, 6)
            for h in range(2):
                sp.dma_start(out[:, h * HD:(h + 1) * HD], t0[h * N:(h + 1) * N, :]).then_inc(out_stored, 16)
            sp.wait_ge(out_stored, 32)

        @block.gpsimd
        def _(pool):
            made = [0]

            def link(ins):
                made[0] += 1
                ins.then_inc(pool_chain, 1)
                pool.wait_ge(pool_chain, made[0])

            link(nc.gpsimd.memset(ident[:, :], 0.0))
            nc.gpsimd.affine_select(out=ident[:, :], in_=ident[:, :], compare_op=ALU.not_equal, fill=1.0,
                                    base=0, pattern=[[-1, P]], channel_multiplier=1).then_inc(ident_ready, 1)
            link(nc.gpsimd.iota(cols_i, pattern=[[1, R * N]], base=0, channel_multiplier=0))
            nc.gpsimd.tensor_copy(cols_f, cols_i).then_inc(consts_ready, 1)
            nc.gpsimd.memset(small[:, 41:42], LN_EPS)
            pool.wait_ge(ident_ready, 1)
            nc.gpsimd.memset(blockd, 0.0).then_inc(consts_ready, 1)
            nc.gpsimd.tensor_copy(adjT[:, R, :], ident[:, :]).then_inc(consts_ready, 1)
            link(nc.gpsimd.tensor_tensor(avg[:, 0:N], ident[:, 0:N], ident[:, N:P], ALU.add))
            link(nc.gpsimd.tensor_scalar(avg[:, 0:N], avg[:, 0:N], 0.5, None, ALU.mult))
            link(nc.gpsimd.tensor_copy(avg[:, N:P], avg[:, 0:N]))
            link(nc.gpsimd.memset(rsel[:, :], 0.0))
            link(nc.gpsimd.memset(rsel[0:L, N - 1:N], 1.0))
            link(nc.gpsimd.memset(rsel[L:P, N - 1 + NB:N + NB], 1.0))
            link(nc.gpsimd.memset(i3[:, :], 0.0))
            for g in range(3):
                rows = i3[g * GN:(g + 1) * GN, :]
                link(nc.gpsimd.affine_select(out=rows, in_=rows, compare_op=ALU.not_equal, fill=1.0, base=0,
                                             pattern=[[-1, GN]], channel_multiplier=1))
            for g in range(PPG):
                rows = i3[:, g * 2 * NB:(g + 1) * 2 * NB].rearrange("p (b n) -> p n b", b=2)
                nc.gpsimd.tensor_copy(bsel[:, g * NB:(g + 1) * NB, :].rearrange("p n (b l) -> p n b l", b=2),
                                      rows.unsqueeze(3).to_broadcast([3 * GN, NB, 2, L])).then_inc(consts_ready, 1)

            nb = len(BIASES)
            link(nc.gpsimd.memset(biases[:, :], 0.0))
            pool.wait_ge(bias_loaded, 16 * nb)
            link(nc.gpsimd.tensor_copy(biases[0:nb, :], bias[:, :]))
            link(nc.gpsimd.tensor_tensor(bias[:, :], bias[:, :], biases[0:nb, :], ALU.subtract))
            link(nc.gpsimd.tensor_copy(bias_mid[:, :], bias[:, :]))
            link(nc.gpsimd.tensor_tensor(bias[:, :], bias[:, :], bias_mid[:, :], ALU.subtract))
            nc.gpsimd.tensor_copy(biases[GN:GN + nb, :], bias_mid[:, :]).then_inc(biases_split, 1)
            nc.gpsimd.tensor_copy(biases[2 * GN:2 * GN + nb, :], bias[:, :]).then_inc(biases_split, 1)

            for layer in range(2):
                for t in range(TILES):
                    T = layer * TILES + t
                    if not on_pool(T):
                        continue
                    pool.wait_ge(sig_ready, T + 1)
                    if T >= PRODS:
                        pool.wait_ge(reduced, T - PRODS + 1)
                    nc.gpsimd.tensor_tensor(prod[:, T % PRODS, :], pre[:, T % PRES, :],
                                            qn[:, t // NB, :], ALU.mult).then_inc(prod_p, 1)

        @block.scalar
        def _(act):
            made = [0]

            def link(ins):
                made[0] += 1
                ins.then_inc(act_chain, 1)
                act.wait_ge(act_chain, made[0])

            for g in range(G_H):
                if group_on_act(g):
                    copy_group(act, g, turned_out_s)
            act.wait_ge(deg_ready, 1)
            nc.scalar.activation(small[:, 9:10], small[:, 8:9], ACT.Sqrt).then_inc(sqrt_deg, 1)
            act.wait_ge(sqrt_deg, 1)
            nc.scalar.activation(small[:, 42:43], small[:, 9:10], ACT.Sigmoid)

            def unit_copy(u):
                act.wait_ge(qg_done, u + 1)
                nc.scalar.copy(qg[:, u // 2, HD:D], ps[:, unit_bank(u), 0:HD]).then_inc(qg_out_s, 1)

            unit_copy(1)
            for g in range(G_H, G_QH):
                if group_on_act(g):
                    copy_group(act, g, turned_out_s)
            for u in range(3, UNITS - 3, 2):
                unit_copy(u)

            def mix_copy(layer):
                act.wait_ge(mixed, 3 * layer + 2)
                nc.scalar.copy(mixT[:, 1, :], ps[:, mix_bank(layer, 1), :]).then_inc(mix_out_s, 1)

            for layer in range(2):
                if layer == 0:
                    unit_copy(UNITS - 3)
                mix_copy(layer)
                if layer == 0:
                    for k in range(len(EARLY)):
                        copy_group(act, G_QH + k, turned_out_s)
                def stack_part(i, g, h):
                    part, stacked = ((hi, hi_stacked), (mid, mid_stacked))[i]
                    nc.scalar.copy(stack[i * GN:(i + 1) * GN, h, g, :],
                                   part[h * N + g * GN:h * N + (g + 1) * GN, :]).then_inc(stacked, 1)

                for i, ready in enumerate((hi_ready, mid_ready)):
                    act.wait_ge(ready, layer + 1)
                    for h in range(2):
                        stack_part(i, 0, h)
                if layer == 0:
                    unit_copy(UNITS - 1)
                    act.wait_ge(qg_out_s, NP)
                for t in range(TILES):
                    T = layer * TILES + t
                    if layer == 0:
                        for k in range(late_groups(t + 1) if t else len(EARLY), late_groups(t + 2)):
                            copy_group(act, G_QH + k, turned_out_s)
                    act.wait_ge(pre_ready, T + 1)
                    if 2 <= t < 6:
                        stack_part((t - 2) // 2, 1, t % 2)
                    src = by_half(pre[:, T % PRES, :])
                    dst = src
                    if not on_pool(T):
                        dst = ps[:, GATE:GATE + 2, 0:HD]
                        if vec_tiles(T):
                            act.wait_ge(prod_v, vec_tiles(T))
                    nc.scalar.activation(dst, src, ACT.Sigmoid).then_inc(sig_ready, 1)
                act.wait_ge(qi_ready, layer + 1)
                nc.scalar.activation(t2[:, :], t0[:, :], ACT.Tanh).then_inc(tanh_ready, 1)
                act.wait_ge(alpha_done, layer + 1)
                nc.scalar.activation(t1[:, :], ps[:, TRB, 0:HD], ACT.Sigmoid).then_inc(alpha_ready, 1)

            def ln(n):
                act.wait_ge(ln_var, n)
                nc.scalar.activation(small[:, 5:6], small[:, 4:5], ACT.Sqrt, bias=small[:, 41:42]).then_inc(ln_std, 1)

            ln(1)
            ln(2)
            for layer in range(2):
                hp = 2 - layer
                act.wait_ge(rel_done, 2 * layer + 1)
                nc.scalar.copy(X2[:, HD:D], ps[N:P, 2, 0:HD]).then_inc(X_out_s, 1)
                act.wait_ge(rel_done, 2 * layer + 2)
                nc.scalar.copy(X01[:, HD:D], ps[:, 1, 0:HD]).then_inc(X_out_s, 1)
                act.wait_ge(X_turned, 3 * layer + 3)
                nc.scalar.copy(XT[:, JC:KC, 0:P], ps[:, 4, 0:HD].rearrange("p (k n) -> p k n", k=JC)).then_inc(XT_out_s, 1)
                act.wait_ge(shifted, layer + 1)
                n = R * N
                for h in range(hp):
                    nc.scalar.activation(expd[:, h * n:(h + 1) * n], leaky[:, h * n:(h + 1) * n], ACT.Exp,
                                         bias=small[:, 16 + h:17 + h]).then_inc(exp_ready, 1)
                act.wait_ge(wts_turned, layer + 1)
                nc.scalar.copy(wT2[:, 0:hp * P], ps[0:N, 7, 0:hp * P]).then_inc(wT_out_s, 1)
                if layer == 0:
                    act.wait_ge(elu_min, 1)
                    nc.scalar.activation(t2[:, :], t2[:, :], ACT.Exp).then_inc(elu_exp, 1)
            ln(3)
            ln(4)

        @block.vector
        def _(dve):
            made = [0]

            def link(ins):
                made[0] += 1
                ins.then_inc(vec_chain, 1)
                dve.wait_ge(vec_chain, made[0])

            dve.wait_ge(edges_loaded, 48)
            link(nc.vector.tensor_copy(edge_f, eidx[:, :, :]))
            link(nc.vector.scalar_tensor_tensor(out=edge_f[:, 0, :], in0=edge_f[:, 2, :], scalar=float(N),
                                                in1=edge_f[:, 0, :], op0=ALU.mult, op1=ALU.add))
            dve.wait_ge(consts_ready, 1)
            nc.vector.tensor_tensor(hot_src, cols_f.unsqueeze(1).to_broadcast([P, EC, R * N]),
                                    edge_f[:, 0, :].unsqueeze(2).to_broadcast([P, EC, R * N]),
                                    ALU.is_equal).then_inc(hot_ready, 1)
            for h in range(2):
                nc.vector.tensor_tensor(hot_dst[:, :, h * N:(h + 1) * N], cols_f[:, 0:N].unsqueeze(1).to_broadcast([P, EC, N]),
                                        edge_f[:, 1, :].unsqueeze(2).to_broadcast([P, EC, N]),
                                        ALU.is_equal).then_inc(hot_ready, 1)
            def copy_groups(gs):
                for g in gs:
                    if not group_on_act(g):
                        copy_group(dve, g, turned_out_v)

            dve.wait_ge(counts_done, 1)
            link(nc.vector.tensor_copy(M[:, :], ps[:, 0, 0:R * N]))
            copy_groups(range(G_H))
            link(nc.vector.tensor_scalar(maskb[:, :], M[:, :], 0.0, NEG, ALU.is_equal, ALU.mult))
            link(nc.vector.tensor_reduce(small[:, 0:R], M[:, :].rearrange("p (r n) -> p r n", r=R), AX.X, ALU.add))
            link(nc.vector.tensor_reduce(small[:, 7:8], small[:, 0:R], AX.X, ALU.add))
            nc.vector.tensor_scalar(small[:, 8:9], small[:, 7:8], 1.0, None, ALU.add).then_inc(deg_ready, 1)
            link(nc.vector.tensor_scalar(small[:, 0:R], small[:, 0:R], 1.0, None, ALU.max))
            link(nc.vector.reciprocal(small[:, 10:10 + R], small[:, 0:R]))
            dve.wait_ge(consts_ready, 3)
            for h in range(2):
                rows = slice(h * N, (h + 1) * N)
                m3 = M[rows, :].rearrange("p (r n) -> p r n", r=R)
                link(nc.vector.tensor_tensor(blockd[rows, 0:R, rows], m3,
                                             small[rows, 10:10 + R].unsqueeze(2).to_broadcast([N, R, N]), ALU.mult))
                link(nc.vector.tensor_reduce(blockd[rows, R, rows], M[rows, :].rearrange("p (r n) -> p n r", r=R),
                                             AX.X, ALU.add))
            link(nc.vector.tensor_tensor(blockd[:, R, :], blockd[:, R, :], ident[:, :], ALU.add))
            dve.wait_ge(sqrt_deg, 1)
            link(nc.vector.reciprocal(small[:, 13:14], small[:, 9:10]))
            nc.vector.tensor_scalar(blockd[:, R, :], blockd[:, R, :], small[:, 13:14], None, ALU.mult).then_inc(blocks_ready, 1)
            def unit_copy(u):
                dve.wait_ge(qg_done, u + 1)
                nc.vector.tensor_copy(qg[:, u // 2, 0:HD], ps[:, unit_bank(u), 0:HD]).then_inc(qg_out_v, 1)

            unit_copy(0)
            copy_groups(range(G_H, G_QH))
            dve.wait_ge(adj_turned, 1)
            nc.vector.tensor_copy(adjT[:, 0:R, :], ps[:, GATE, 0:R * P].rearrange("p (r n) -> p r n", r=R)).then_inc(adj_ready, 1)
            nc.vector.tensor_scalar(gcnT[:, :], ps[:, GATE, R * P:(R + 1) * P], small[:, 13:14], None, ALU.mult).then_inc(adj_ready, 1)
            for u in range(2, UNITS - 2, 2):
                unit_copy(u)

            def layer_norm(y, dst, n):
                link(nc.vector.bn_stats(small[:, 20:26], y))
                nc.vector.bn_aggr(small[:, 0:2], small[:, 20:26]).then_inc(ln_parts, 1)
                dve.wait_ge(ln_mean, n)
                dve.wait_ge(ln_parts, n)
                link(nc.vector.tensor_tensor(small[:, 6:7], small[:, 0:1], ps[:, TRB, 0:1], ALU.subtract))
                nc.vector.scalar_tensor_tensor(out=small[:, 4:5], in0=small[:, 6:7], scalar=small[:, 6:7],
                                               in1=ps[:, TRB, 1:2], op0=ALU.mult, op1=ALU.add).then_inc(ln_var, 1)
                link(nc.vector.tensor_copy(small[:, 2:3], ps[:, TRB, 0:1]))
                dve.wait_ge(ln_std, n)
                link(nc.vector.reciprocal(small[:, 6:7], small[:, 5:6]))
                nc.vector.tensor_scalar(dst, y, small[:, 2:3], small[:, 6:7], ALU.subtract, ALU.mult).then_inc(x_ready, 1)

            for layer in range(2):
                for i, j in enumerate((0, 2)):
                    dve.wait_ge(mixed, 3 * layer + j + 1)
                    nc.vector.tensor_copy(mixT[:, j, :], ps[:, mix_bank(layer, j), :]).then_inc(mix_out_v, 1)
                if layer == 0:
                    unit_copy(UNITS - 2)
                dve.wait_ge(rgcn_done, (R + 1) * (layer + 1))
                nc.vector.tensor_scalar(hh[:, :], ps[:, ACC, 0:HD], 0.0, None, ALU.max).then_inc(h_ready, 1)
                dve.wait_ge(node_turned, layer + 1)
                nc.vector.tensor_copy(nodeT[:, :, :], ps[:, 3, 0:HD].rearrange("p (j n) -> p j n", j=JC)).then_inc(nodeT_ready, 1)
                dve.wait_ge(hg_done, layer + 1)
                nc.vector.tensor_copy(hi[:, :], ps[:, HG, 0:HD]).then_inc(hi_ready, 1)
                dve.wait_ge(hi_ready, layer + 1)
                link(nc.vector.tensor_tensor(t1[:, :], ps[:, HG, 0:HD], hi[:, :], ALU.subtract))
                nc.vector.tensor_copy(mid[:, :], t1[:, :]).then_inc(mid_ready, 1)
                dve.wait_ge(mid_ready, layer + 1)

                def stack_low(g, h):
                    r = slice(h * N + g * GN, h * N + (g + 1) * GN)
                    nc.vector.tensor_tensor(stack[2 * GN:3 * GN, h, g, :], t1[r, :], mid[r, :],
                                            ALU.subtract).then_inc(lo_stacked, 1)

                for h in range(2):
                    stack_low(0, h)
                LAG = 2
                for t in range(TILES + LAG):
                    T = layer * TILES + t
                    if 2 <= t < 4:
                        stack_low(1, t % 2)
                    if t == (NP - 1) * NB:
                        wait_units_out(dve, UNITS)
                    elif t == 0:
                        wait_units_out(dve, UNITS - 1)
                    if t < TILES:
                        dve.wait_ge(hg_cast, T + 1)
                        if T >= PRES:
                            if on_pool(T - PRES):
                                dve.wait_ge(prod_p, pool_tiles(T - PRES + 1))
                            else:
                                dve.wait_ge(sig_ready, T - PRES + 1)
                        nc.vector.tensor_tensor(by_half(pre[:, T % PRES, :]), ring(T), by_half(qg[:, t // NB, :]),
                                                ALU.add).then_inc(pre_ready, 1)
                    if t >= LAG and not on_pool(T - LAG):
                        T -= LAG
                        dve.wait_ge(sig_ready, T + 1)
                        if T >= PRODS:
                            dve.wait_ge(reduced, T - PRODS + 1)
                        nc.vector.tensor_tensor(by_half(prod[:, T % PRODS, :]), ps[:, GATE:GATE + 2, 0:HD],
                                                by_half(qn[:, (t - LAG) // NB, :]), ALU.mult).then_inc(prod_v, 1)
                dve.wait_ge(reduced, (layer + 1) * TILES)
                nc.vector.tensor_copy(t0[:, :], ps[:, ACC, 0:HD]).then_inc(qi_ready, 1)
                dve.wait_ge(qi_turned, layer + 1)
                nc.vector.tensor_copy(qiT[:, :, :], ps[:, 0, 0:HD].rearrange("p (j n) -> p j n", j=JC)).then_inc(qiT_ready, 1)
                dve.wait_ge(tanh_ready, layer + 1)
                link(nc.vector.tensor_tensor(t2[:, :], t2[:, :], hh[:, :], ALU.subtract))
                if layer == 1:
                    link(nc.vector.tensor_tensor(hh[:, :], hh[:, :], xa[:, :], ALU.add))
                dve.wait_ge(alpha_ready, layer + 1)
                link(nc.vector.tensor_tensor(t1[:, :], t1[:, :], t2[:, :], ALU.mult))
                if layer == 0:
                    nc.vector.tensor_tensor(hx[:, :], t1[:, :], hh[:, :], ALU.add).then_inc(x_ready, 1)
                else:
                    link(nc.vector.tensor_tensor(t0[:, :], t1[:, :], hh[:, :], ALU.add))
            layer_norm(t0[:, :], xa[:, :], 1)

            def gcn_mix(n):
                dve.wait_ge(node_turned, n)
                nc.vector.tensor_copy(nodeT[:, :, :], ps[:, 3, 0:HD].rearrange("p (j n) -> p j n", j=JC)).then_inc(nodeT_ready, 1)

            gcn_mix(3)
            dve.wait_ge(proj_done, 1)
            layer_norm(ps[:, ACC, 0:HD], xa[:, :], 2)

            for layer in range(2):
                hp = 2 - layer
                bw = HD // hp
                n = R * N
                gcn_mix(4 + layer)
                dve.wait_ge(rel_done, 2 * layer + 1)
                nc.vector.tensor_copy(X2[:, 0:HD], ps[0:N, 2, 0:HD]).then_inc(X_out_v, 1)
                dve.wait_ge(X_turned, 3 * layer + 1)
                nc.vector.tensor_copy(XT[:, :, P:n], ps[:, 5, 0:HD].rearrange("p (k n) -> p k n", k=KC)).then_inc(XT_out_v, 1)
                dve.wait_ge(rel_done, 2 * layer + 2)
                nc.vector.tensor_copy(X01[:, 0:HD], ps[:, 0, 0:HD]).then_inc(X_out_v, 1)
                dve.wait_ge(X_turned, 3 * layer + 2)
                nc.vector.tensor_copy(XT[:, 0:JC, 0:P], ps[:, 3, 0:HD].rearrange("p (k n) -> p k n", k=JC)).then_inc(XT_out_v, 1)
                dve.wait_ge(qk_done, layer + 1)
                nc.vector.tensor_copy(QKT[0:4 * hp if hp == 2 else 2, :], ps[0:4 * hp if hp == 2 else 2, 6, 0:n]).then_inc(qkT_ready, 1)
                dve.wait_ge(score_done, layer + 1)
                link(nc.vector.tensor_copy(score[:, 0:hp * n], ps[:, 0, 0:hp * n]))
                link(nc.vector.scalar_tensor_tensor(out=leaky[:, 0:hp * n], in0=score[:, 0:hp * n], scalar=SLOPE,
                                                    in1=score[:, 0:hp * n], op0=ALU.mult, op1=ALU.max))
                nc.vector.tensor_reduce(small[:, 16:16 + hp], leaky[:, 0:hp * n].rearrange("p (h c) -> p h c", h=hp),
                                        AX.X, ALU.max, negate=True).then_inc(shifted, 1)
                for h in range(hp):
                    dve.wait_ge(exp_ready, 2 * layer + h + 1)
                    nc.vector.tensor_tensor_reduce(wts[:, h * n:(h + 1) * n], expd[:, h * n:(h + 1) * n], M[:, :], 1.0, 0.0,
                                                   ALU.mult, ALU.add, small[:, 18 + h:19 + h]).then_inc(wts_ready, 1)
                dve.wait_ge(wts_turned, layer + 1)
                nc.vector.tensor_copy(wT1[:, 0:hp * P], ps[:, 3, 0:hp * P]).then_inc(wT_out_v, 1)
                link(nc.vector.tensor_scalar(small[:, 18:18 + hp], small[:, 18:18 + hp], SOFTMAX_EPS, None, ALU.add))
                link(nc.vector.reciprocal(small[:, 32:32 + hp], small[:, 18:18 + hp]))
                dve.wait_ge(addend_done, layer + 1)
                link(nc.vector.tensor_copy(t1[:, :], ps[:, ADDEND, 0:HD]))
                dve.wait_ge(att_done, layer + 1)
                for h in range(hp):
                    ins = nc.vector.scalar_tensor_tensor(out=t0[:, h * bw:(h + 1) * bw], in0=ps[:, ACC, h * bw:(h + 1) * bw],
                                                         scalar=small[:, 32 + h:33 + h], in1=t1[:, h * bw:(h + 1) * bw],
                                                         op0=ALU.mult, op1=ALU.add)
                    link(ins)
                if layer == 0:
                    nc.vector.tensor_scalar(t2[:, :], t0[:, :], 0.0, None, ALU.min).then_inc(elu_min, 1)
                    link(nc.vector.tensor_scalar(t0[:, :], t0[:, :], 0.0, None, ALU.max))
                    dve.wait_ge(elu_exp, 1)
                    nc.vector.scalar_tensor_tensor(out=hx[:, :], in0=t2[:, :], scalar=-1.0, in1=t0[:, :],
                                                   op0=ALU.add, op1=ALU.add).then_inc(x_ready, 1)
                else:
                    layer_norm(t0[:, :], xa[:, :], 3)
            gcn_mix(6)
            dve.wait_ge(proj_done, 2)
            nc.vector.tensor_scalar(hx[:, :], ps[:, ACC, 0:HD], 0.0, None, ALU.max).then_inc(y_ready, 1)
            gcn_mix(7)
            dve.wait_ge(proj_done, 3)
            layer_norm(ps[:, LAST, 0:HD], t0[:, :], 4)

        @block.tensor
        def _(pe):
            def turn_blocks(g, blocks):
                at = 0
                for src in blocks:
                    ins = nc.tensor.transpose(ps[:, group_bank(g), at:at + P], src, ident[:, :])
                    at += P
                ins.then_inc(turned, 1)

            def turn_weight(g0, key, k):
                part, col = k // KC, k % KC
                if col == 0:
                    wait_loaded(pe, key, part)
                if g0 < G_QH:
                    if g0 + k >= 4:
                        wait_group_out(pe, g0 + k - 4)
                elif g0 + k >= G_QH + len(EARLY):
                    wait_group_out(pe, g0 + k - 1)
                src = W[SLOT[key]]
                turn_blocks(g0 + k, [src[:, part * JC + i, col * P:(col + 1) * P] for i in range(JC)])

            def project(T, w, bank, first=True, last=True, col0=0, chunks=range(KC)):
                for k in chunks:
                    h, j = k // JC, k % JC
                    for c in range(2):
                        ins = nc.tensor.matmul(ps[c * N:(c + 1) * N, bank, 0:HD],
                                               T[:, j, col0 + h * N:col0 + (h + 1) * N],
                                               w[:, k, c * HD:(c + 1) * HD],
                                               start=(first and k == 0), stop=(last and k == KC - 1),
                                               skip_group_check=True)
                return ins

            def add_nodes(x, bank):
                for c in range(2):
                    ins = nc.tensor.matmul(ps[c * N:(c + 1) * N, bank, 0:HD], ident[:, c * N:(c + 1) * N],
                                           x[:, :], start=False, stop=False, skip_group_check=True)
                return ins

            def add_bias(name, bank):
                i = BIASES.index(name)
                for c in range(2):
                    ins = nc.tensor.matmul(ps[c * N:(c + 1) * N, bank, 0:HD],
                                           i3[:, i:i + 1].to_broadcast([3 * GN, N]),
                                           biases[:, c * HD:(c + 1) * HD], start=True, stop=False, skip_group_check=True)
                return ins

            def turn_nodes(y, bank, right):
                for j in range(JC):
                    out_j = ps[:, bank, j * P:(j + 1) * P]
                    if right is ident:
                        ins = nc.tensor.transpose(out_j, y[:, j * P:(j + 1) * P], ident[:, :])
                    else:
                        ins = nc.tensor.matmul(out_j, y[:, j * P:(j + 1) * P], right[:, :], start=True, stop=True)
                return ins

            def keep_warm(n, bank):
                for _ in range(n):
                    nc.tensor.matmul(ps[:, bank, :], bsel[:, 0, :], bsel[:, 0:4, :].rearrange("p a b -> p (a b)"),
                                     start=True, stop=True, skip_group_check=True)

            pe.wait_ge(hot_ready, 3)
            for c in range(EC):
                ins = nc.tensor.matmul(ps[:, 0, 0:R * N], hot_dst[:, c, :], hot_src[:, c, :],
                                       start=(c == 0), stop=(c == EC - 1))
            ins.then_inc(counts_done, 1)
            pe.wait_ge(ident_ready, 1)
            for k in range(GROUPS):
                turn_weight(0, "Wg_q", k)
            pe.wait_ge(q_loaded, 32)
            for k in range(NQG):
                wait_group_out(pe, G_Q + k - 4)
                turn_blocks(G_Q + k, [qn[:, p, k * P:(k + 1) * P] for p in range(NP)])
            def query_unit(u):
                if 4 <= u < UNITS - 1:
                    wait_units_out(pe, u - 3)
                p, c = u // 2, u % 2
                for k in range(KC):
                    ins = nc.tensor.matmul(ps[:, unit_bank(u), 0:HD], qT[:, k, p * P:(p + 1) * P],
                                           WgT_q[:, k, c * HD:(c + 1) * HD], start=(k == 0), stop=(k == KC - 1))
                ins.then_inc(qg_done, 1)

            def turn_wq(ks):
                for k in ks:
                    turn_weight(G_QH + (k // GROUPS) * GROUPS, ("Wq_h", "Wq_q")[k // GROUPS], k % GROUPS)

            def mix(layer, x):
                for j in range(JC):
                    nc.tensor.matmul(ps[:, mix_bank(layer, j), :], x[:, j * P:(j + 1) * P],
                                     adjT[:, :, :].rearrange("p r n -> p (r n)"),
                                     start=True, stop=True).then_inc(mixed, 1)

            for u in range(UNITS - 1):
                if u == 0:
                    wait_groups_out(pe, G_H)
                if u == 2:
                    for k in range(GROUPS):
                        turn_weight(G_H, "Wg_h", k)
                    wait_groups_out(pe, G_QH)
                    pe.wait_ge(blocks_ready, 1)
                    for r in range(R + 1):
                        ins = nc.tensor.transpose(ps[:, GATE, r * P:(r + 1) * P], blockd[:, r, :], ident[:, :])
                    ins.then_inc(adj_turned, 1)
                if u == UNITS - 2:
                    pe.wait_ge(x_loaded, 32)
                    pe.wait_ge(adj_ready, 2)
                    mix(0, xa)
                query_unit(u)

            def gate(layer):
                if layer == 0:
                    pe.wait_ge(consts_ready, 5)
                LAG = 5
                for t in range(TILES + LAG):
                    T = layer * TILES + t
                    if t % (PPG * NB) == 0 and t < TILES:
                        g = t // (PPG * NB)
                        pe.wait_ge(hi_stacked, 4 * layer + 2 * (g + 1))
                        pe.wait_ge(mid_stacked, 4 * layer + 2 * (g + 1))
                        pe.wait_ge(lo_stacked, 4 * layer + 2 * (g + 1))
                    if t < TILES:
                        if T >= RING:
                            pe.wait_ge(pre_ready, T - RING + 1)
                        p, n = t // NB, t % NB
                        for c in range(2):
                            ins = nc.tensor.matmul(ring(T)[:, c, :], bsel[:, (p % PPG) * NB + n, :],
                                                   stack[:, c, p // PPG, :], start=True, stop=True)
                        ins.then_inc(hg_cast, 1)
                    if layer == 0 and t < TILES:
                        turn_wq(range(late_groups(t), late_groups(t + 1)))
                    if t in ALPHA_AT[layer]:
                        if layer == 0 and ALPHA_AT[layer][t] == 0:
                            wait_groups_out(pe, G_END)
                        if ALPHA_AT[layer][t] == 0:
                            add_bias("L0_gnn_bq", TRB)
                        project(nodeT, WqT_h, TRB, first=False, last=False, chunks=[ALPHA_AT[layer][t]])
                    if t >= LAG:
                        T -= LAG
                        if on_pool(T):
                            pe.wait_ge(prod_p, pool_tiles(T + 1))
                        else:
                            pe.wait_ge(prod_v, vec_tiles(T + 1))
                        s = N - 1 - (2 * NB * ((t - LAG) // NB) + (t - LAG) % NB)
                        for c in range(2):
                            ins = nc.tensor.matmul(ps[c * N:(c + 1) * N, ACC, 0:HD], rsel[:, s:s + N],
                                                   prod[:, T % PRODS, c * HD:(c + 1) * HD],
                                                   start=(t == LAG), stop=(t == TILES + LAG - 1), skip_group_check=True)
                        ins.then_inc(reduced, 1)

            for layer in range(2):
                if layer == 1:
                    pe.wait_ge(x_ready, 1)
                    mix(1, hx)
                pe.wait_ge(mix_out_v, 2 * (layer + 1))
                pe.wait_ge(mix_out_s, layer + 1)
                if layer == 0:
                    pe.wait_ge(biases_split, 2)
                add_bias(f"L0_gnn_b{layer + 1}", ACC)
                for r in range(R + 1):
                    key = f"rel{layer + 1}_{r}" if r < R else f"root{layer + 1}"
                    wait_loaded(pe, key)
                    project(mixT, W[SLOT[key]], ACC, first=False, last=(r == R),
                            col0=r * P).then_inc(rgcn_done, 1)
                if layer == 0:
                    wait_units_out(pe, UNITS - 1)
                    turn_wq(range(0, 3))
                pe.wait_ge(h_ready, layer + 1)
                turn_nodes(hh, 3, ident).then_inc(node_turned, 1)
                if layer == 0:
                    turn_wq(range(3, len(EARLY)))
                add_bias("L0_gnn_bg", HG)
                pe.wait_ge(nodeT_ready, layer + 1)
                project(nodeT, WgT_h, HG, first=False).then_inc(hg_done, 1)
                if layer == 1:
                    keep_warm(8, 5)
                if layer == 0:
                    wait_groups_out(pe, G_QH + len(EARLY))
                    query_unit(UNITS - 1)
                gate(layer)
                keep_warm(2, 1)
                pe.wait_ge(qi_ready, layer + 1)
                turn_nodes(t0, 0, ident).then_inc(qi_turned, 1)
                keep_warm(2, 1)
                pe.wait_ge(qiT_ready, layer + 1)
                project(qiT, WqT_q, TRB, first=False).then_inc(alpha_done, 1)
                keep_warm(6 if layer == 0 else 12, 4)

            def norm_stats(n, name=None):
                if n > 1:
                    keep_warm(5, 4)
                pe.wait_ge(ln_parts, n)
                nc.tensor.matmul(ps[:, TRB, 0:2], avg[:, :], small[:, 0:2], start=True, stop=True).then_inc(ln_mean, 1)
                if name is not None:
                    add_bias(name, ACC)
                keep_warm(4, 4)

            def gcn(n, key, x, bank, residual=None):
                turn_nodes(x, 3, gcnT).then_inc(node_turned, 1)
                if residual is not None:
                    add_nodes(residual, bank)
                else:
                    keep_warm(2, 4)
                pe.wait_ge(nodeT_ready, n)
                wait_loaded(pe, key)
                project(nodeT, W[SLOT[key]], bank, first=False).then_inc(proj_done, 1)

            norm_stats(1, "L1_gnn_b")
            pe.wait_ge(x_ready, 2)
            gcn(3, "L1_W", xa, ACC, xa)
            norm_stats(2)

            pe.wait_ge(qk_loaded, 64)
            for layer in range(2):
                hp = 2 - layer
                bw = HD // hp
                m = 4 * hp if hp == 2 else 2
                n = R * N
                x = xa if layer == 0 else hx
                pe.wait_ge(x_ready, 3 + layer)
                turn_nodes(x, 3, ident).then_inc(node_turned, 1)
                keep_warm(2, 4)
                pe.wait_ge(nodeT_ready, 4 + layer)
                keys = [f"L2_W{layer + 1}_{r}" for r in range(R)]
                wait_loaded(pe, keys[2])
                project(nodeT, W[SLOT[keys[2]]], 2).then_inc(rel_done, 1)
                wait_loaded(pe, keys[0])
                wait_loaded(pe, keys[1])
                for k in range(KC):
                    h, j = k // JC, k % JC
                    for c in range(2):
                        for r in range(2):
                            ins = nc.tensor.matmul(ps[r * N:(r + 1) * N, c, 0:HD], nodeT[:, j, h * N:(h + 1) * N],
                                                   W[SLOT[keys[r]]][:, k, c * HD:(c + 1) * HD],
                                                   start=(k == 0), stop=(k == KC - 1), skip_group_check=True)
                    if k == 2:
                        pe.wait_ge(X_out_v, 2 * layer + 1)
                        pe.wait_ge(X_out_s, 2 * layer + 1)
                        for i in range(KC):
                            turn = nc.tensor.transpose(ps[:, 5, i * N:(i + 1) * N], X2[:, i * P:(i + 1) * P],
                                                       ident[0:N, 0:N])
                        turn.then_inc(X_turned, 1)
                ins.then_inc(rel_done, 1)
                keep_warm(1, 4)
                for part in range(2):
                    pe.wait_ge((X_out_v, X_out_s)[part], 2 * layer + 2)
                    for i in range(JC):
                        k = part * JC + i
                        ins = nc.tensor.transpose(ps[:, 3 + part, i * P:(i + 1) * P], X01[:, k * P:(k + 1) * P], ident[:, :])
                    ins.then_inc(X_turned, 1)
                pe.wait_ge(XT_out_v, 2 * layer + 2)
                pe.wait_ge(XT_out_s, layer + 1)
                for k in range(KC):
                    ins = nc.tensor.matmul(ps[0:m, ACC, 0:n], (qk, qk2)[layer][:, k, 0:m], XT[:, k, :],
                                           start=(k == 0), stop=(k == KC - 1))
                ins.then_inc(qk_done, 1)
                nc.tensor.matmul(ps[:, 0, 0:hp * n].rearrange("p (h c) -> p h c", h=hp), ident[:, :],
                                 maskb[:, :].unsqueeze(1).to_broadcast([P, hp, n]), start=True, stop=False,
                                 skip_group_check=True)
                pe.wait_ge(qkT_ready, layer + 1)
                for h in range(hp):
                    for half in range(2):
                        head = hp * half + h if hp == 2 else 0
                        rows = slice(half * N, (half + 1) * N)
                        nc.tensor.matmul(ps[rows, 0, h * n:(h + 1) * n],
                                         ident[0:m, m // 2 + head:m // 2 + head + 1].to_broadcast([m, N]), QKT[0:m, :],
                                         start=False, stop=False, skip_group_check=True)
                for h in range(hp):
                    for r in range(R):
                        for half in range(2):
                            head = hp * half + h if hp == 2 else 0
                            ins = nc.tensor.matmul(ps[half * N:(half + 1) * N, 0, h * n + r * N:h * n + (r + 1) * N],
                                                   QKT[0:m, r * N:(r + 1) * N],
                                                   ident[0:m, head:head + 1].to_broadcast([m, N]),
                                                   start=False, stop=True, skip_group_check=True)
                ins.then_inc(score_done, 1)
                ins = add_bias(f"L2_gnn_b{layer + 1}", ADDEND)
                if layer == 1:
                    ins = add_nodes(xa, ADDEND)
                ins.then_inc(addend_done, 1)
                keep_warm(9, 4)
                pe.wait_ge(wts_ready, 2 * layer + hp)
                for h in range(hp):
                    nc.tensor.transpose(ps[:, 3, h * P:(h + 1) * P], wts[:, h * n:h * n + P], ident[:, :])
                for h in range(hp):
                    ins = nc.tensor.transpose(ps[0:N, 7, h * P:(h + 1) * P], wts[:, h * n + P:(h + 1) * n], ident[:, :])
                ins.then_inc(wts_turned, 1)
                keep_warm(1, 4)
                pe.wait_ge(wT_out_v, layer + 1)
                pe.wait_ge(wT_out_s, layer + 1)
                for h in range(hp):
                    for half in range(2):
                        at = half * HD + h * bw
                        nc.tensor.matmul(ps[half * N:(half + 1) * N, ACC, h * bw:(h + 1) * bw],
                                         wT1[:, h * P + half * N:h * P + (half + 1) * N], X01[:, at:at + bw],
                                         start=True, stop=False, skip_group_check=True)
                        ins = nc.tensor.matmul(ps[half * N:(half + 1) * N, ACC, h * bw:(h + 1) * bw],
                                               wT2[:, h * P + half * N:h * P + (half + 1) * N], X2[:, at:at + bw],
                                               start=False, stop=True, skip_group_check=True)
                ins.then_inc(att_done, 1)
                if layer == 0:
                    keep_warm(8, 4)
            norm_stats(3, "L3_gnn_b1")
            pe.wait_ge(x_ready, 5)
            gcn(6, "L3_W1", xa, ACC)
            add_bias("L3_gnn_b2", LAST)
            keep_warm(1, 4)
            pe.wait_ge(y_ready, 1)
            gcn(7, "L3_W2", hx, LAST, xa)
            norm_stats(4)


def kernel(**inputs):
    import numpy as _np
    import concourse.bacc as _bacc
    from concourse import mybir as _mybir
    from concourse.bass_utils import run_bass_kernel_spmd as _run

    nc = _bacc.Bacc("TRN2", target_bir_lowering=False, num_devices=1)
    arrays, aps = {}, {}
    for name, value in inputs.items():
        v = _np.ascontiguousarray(value)
        arrays[f"in_{name}"] = v
        aps[name] = nc.dram_tensor(f"in_{name}", v.shape, _mybir.dt.from_np(v.dtype), kind="ExternalInput").ap()
    shape = arrays["in_x"].shape
    out = nc.dram_tensor("out", shape, _mybir.dt.float32, kind="ExternalOutput").ap()
    gnn_kernel(nc, aps, out)
    r = _run(nc, [arrays], core_ids=[0])
    return r.results[0]["out"]
```

```python
from contextlib import ExitStack

import concourse.bass as bass
from concourse import mybir

ALU = mybir.AluOpType
ACT = mybir.ActivationFunctionType
AX = mybir.AxisListType
F32 = mybir.dt.float32
BF16 = mybir.dt.bfloat16
I32 = mybir.dt.int32

P = 128
NEG = -1.0e30
LN_EPS = 1e-5
SOFTMAX_EPS = 1e-16
SLOPE = 0.2


def gnn_kernel(nc: bass.Bass, a, out):
    N, D = a["x"].shape
    E = a["src"].shape[0]
    R = a["L0_gnn_W_rel1"].shape[0]
    B, L, _ = a["L0_gnn_query_embs"].shape
    NB = N // B
    HD = D // 2
    QW = D // 4
    KC = D // P
    JC = KC // 2
    EC = E // P
    NP = B // 2
    TILES = NP * NB
    GN = 32
    PPG = GN // (2 * NB)
    assert N == 64 and 2 * L == P and 2 * HD == D and KC % 2 == 0


    PLAN = [("Wg_q", 0, 2), ("Wg_h", 3, 2), ("rel1_0", 5, 1), ("rel1_1", 6, 1), ("rel1_2", 0, 1), ("root1", 3, 1),
            ("Wq_h", 5, 2), ("Wq_q", 6, 2), ("rel2_0", 3, 1), ("rel2_1", 2, 1), ("rel2_2", 5, 1), ("root2", 6, 1),
            ("L1_W", 3, 1), ("L2_W1_0", 2, 1), ("L2_W1_1", 5, 1), ("L2_W1_2", 6, 1),
            ("L2_W2_0", 4, 1), ("L2_W2_1", 0, 1), ("L2_W2_2", 1, 1), ("L3_W1", 3, 1), ("L3_W2", 2, 1)]
    SLOT = {key: s for key, s, _ in PLAN}
    PARTS = {key: n for key, _, n in PLAN}

    with ExitStack() as ctx:
        def sb(name, shape, dt=F32):
            return ctx.enter_context(nc.sbuf_tensor(name, shape, dt))

        def sem(name):
            return ctx.enter_context(nc.semaphore(name))

        NSLOT = 7
        W = [sb(f"W{s}", [P, KC, D]) for s in range(NSLOT)]
        qn = sb("qn", [P, NP, D])
        qg = sb("qg", [P, NP, D])
        PRODS = 4
        prod = sb("prod", [P, PRODS, D])
        PRES = 4
        pre = sb("pre", [P, PRES, D])
        BIASES = ["L0_gnn_b1", "L0_gnn_b2", "L0_gnn_bg", "L0_gnn_bq", "L1_gnn_b", "L2_gnn_b1", "L2_gnn_b2",
                  "L3_gnn_b1", "L3_gnn_b2"]
        bias = sb("bias", [len(BIASES), D])
        bias_mid = sb("bias_mid", [len(BIASES), D], BF16)
        biases = sb("biases", [3 * GN, D], BF16)
        nodeT = sb("nodeT", [P, JC, P])
        adjT = sb("adjT", [P, R + 1, P])
        gcnT = sb("gcnT", [P, P])
        ident = sb("ident", [P, P])
        avg = sb("avg", [P, P])
        bsel = sb("bsel", [3 * GN, PPG * NB, P], BF16)
        i3 = sb("i3", [3 * GN, GN], BF16)
        rsel = sb("rsel", [P, N])
        stack = sb("stack", [3 * GN, 2, 2, HD], BF16)
        xa = sb("xa", [P, HD])
        hh = sb("hh", [P, HD])
        hx = sb("hx", [P, HD])
        t0 = sb("t0", [P, HD])
        t1 = sb("t1", [P, HD])
        t2 = sb("t2", [P, HD])
        hi = sb("hi", [P, HD], BF16)
        mid = sb("mid", [P, HD], BF16)
        M = sb("M", [P, R * N])
        maskb = sb("maskb", [P, R * N])
        small = sb("small", [P, 64])
        eidx = sb("eidx", [P, 3, EC], I32)
        qk = sb("qk", [P, KC, 2, GN])
        qsel = sb("qsel", [P, GN])

        prod_f = prod[:, :, :].rearrange("p a b -> p (a b)")
        hot_src = prod_f[:, 0:EC * R * N // 2].bitcast(BF16).rearrange("p (c k) -> p c k", c=EC)
        o = EC * R * N // 2
        hot_dst = prod_f[:, o:o + EC * P // 2].bitcast(BF16).rearrange("p (c k) -> p c k", c=EC)
        o += EC * P // 2
        blockd = prod_f[:, o:o + (R + 1) * P].rearrange("p (r k) -> p r k", r=R + 1)
        mixT = prod_f[:, 0:JC * (R + 1) * P].rearrange("p (j n) -> p j n", j=JC)
        qiT = prod_f[:, JC * (R + 1) * P:JC * (R + 2) * P].rearrange("p (j n) -> p j n", j=JC)
        pre_f = pre[:, :, :].rearrange("p a b -> p (a b)")
        cols_i = pre_f[:, 0:R * N].bitcast(I32)
        cols_f = pre_f[:, R * N:2 * R * N]
        edge_f = pre_f[:, 2 * R * N:2 * R * N + 3 * EC].rearrange("p (a c) -> p a c", a=3)
        qT = W[2][:, :, 0:NP * P]
        qn_f = qn[:, :, :].rearrange("p a b -> p (a b)")
        qg_f = qg[:, :, :].rearrange("p a b -> p (a b)")
        X01 = qn_f[:, 0:D]
        X2 = qn_f[0:N, D:2 * D]
        XT = qn_f[:, 2 * D:2 * D + KC * R * N].rearrange("p (k n) -> p k n", k=KC)
        score = qg_f[:, 0:HD]
        leaky = qg_f[:, HD:2 * HD]
        expd = qg_f[:, 2 * HD:3 * HD]
        wts = qg_f[:, 3 * HD:4 * HD]
        wT1 = qg_f[:, 4 * HD:4 * HD + 2 * P]
        wT2 = qg_f[0:N, 4 * HD + 2 * P:4 * HD + 4 * P]
        QKT = qg_f[:, 6 * HD:6 * HD + R * N]

        ps = ctx.enter_context(nc.psum_tensor("ps", [P, 8, 512], F32))
        RING = (2, 3)
        TRA, ACC, TRB = 4, 6, 7
        HG = (4, 6)
        ADDEND = 5
        LAST = 5

        BLOCKS = (slice(0, P), slice(P, HD))
        NODE_BANKS = (3, 1)

        def ring(T):
            s = 2 * (T % TILES % RING[T // TILES])
            return ps[:, s:s + 2, 0:HD]

        def by_half(tile):
            return tile.rearrange("p (h f) -> p h f", h=2)

        loaded = {key: [sem(f"{key}_{c}_loaded") for c in range(n)] for key, _, n in PLAN}
        edges_loaded = sem("edges_loaded")
        x_loaded = sem("x_loaded")
        q_loaded = sem("q_loaded")
        qk_cleared = sem("qk_cleared")
        qk_loaded = sem("qk_loaded")
        bias_loaded = sem("bias_loaded")
        out_stored = sem("out_stored")
        pool_chain = sem("pool_chain")
        vec_chain = sem("vec_chain")
        act_chain = sem("act_chain")
        ident_ready = sem("ident_ready")
        consts_ready = sem("consts_ready")
        hot_ready = sem("hot_ready")
        counts_done = sem("counts_done")
        blocks_ready = sem("blocks_ready")
        adj_turned = sem("adj_turned")
        adj_ready = sem("adj_ready")
        deg_ready = sem("deg_ready")
        sqrt_deg = sem("sqrt_deg")
        turned = sem("turned")
        turned_out_v = sem("turned_out_v")
        turned_out_s = sem("turned_out_s")
        qg_done = sem("qg_done")
        qg_out_v = sem("qg_out_v")
        qg_out_s = sem("qg_out_s")
        mixed = sem("mixed")
        mix_out_v = sem("mix_out_v")
        mix_out_s = sem("mix_out_s")
        rgcn_done = sem("rgcn_done")
        h_ready = sem("h_ready")
        node_turned = sem("node_turned")
        nodeT_ready = sem("nodeT_ready")
        hg_done = sem("hg_done")
        hi_ready = sem("hi_ready")
        mid_ready = sem("mid_ready")
        hi_stacked = sem("hi_stacked")
        mid_stacked = sem("mid_stacked")
        lo_stacked = sem("lo_stacked")
        hg_cast = sem("hg_cast")
        pre_ready = sem("pre_ready")
        sig_ready = sem("sig_ready")
        prod_v = sem("prod_v")
        prod_p = sem("prod_p")
        reduced = sem("reduced")
        qi_out_v = sem("qi_out_v")
        qi_out_s = sem("qi_out_s")
        tanh_ready = sem("tanh_ready")
        qi_turned = sem("qi_turned")
        qiT_ready = sem("qiT_ready")
        alpha_done = sem("alpha_done")
        alpha_ready = sem("alpha_ready")
        x_ready = sem("x_ready")
        ln_parts = sem("ln_parts")
        ln_mean = sem("ln_mean")
        ln_var = sem("ln_var")
        ln_std = sem("ln_std")
        proj_done = sem("proj_done")
        rel_done = sem("rel_done")
        X_out_v = sem("X_out_v")
        X_out_s = sem("X_out_s")
        X_turned = sem("X_turned")
        XT_out_v = sem("XT_out_v")
        XT_out_s = sem("XT_out_s")
        qk_done = sem("qk_done")
        qkT_ready = sem("qkT_ready")
        score_done = sem("score_done")
        shifted = sem("shifted")
        exp_ready = sem("exp_ready")
        wts_ready = sem("wts_ready")
        wts_turned = sem("wts_turned")
        wT_out_v = sem("wT_out_v")
        wT_out_s = sem("wT_out_s")
        biases_split = sem("biases_split")
        addend_done = sem("addend_done")
        att_done = sem("att_done")
        elu_min = sem("elu_min")
        elu_exp = sem("elu_exp")
        y_ready = sem("y_ready")

        TENSOR_ADDS = [TILES + t for t in (0, 1, 7, 13, 19, 25, 30)]
        AHEAD = TENSOR_ADDS[:2]

        def vec_adds(T):
            return T - sum(k < T for k in TENSOR_ADDS)

        POOL_TILES = [t * 3 // 2 for t in range(20)] + [TILES + t * 8 // 5 for t in range(19)]

        def on_pool(T):
            return T in POOL_TILES

        def pool_tiles(T):
            return sum(on_pool(k) for k in range(T))

        def vec_tiles(T):
            return T - pool_tiles(T)

        GROUPS = 2 * KC

        def group_on_act(g):
            return g >= G_QH or g % 2 == 0

        G_Q = GROUPS
        NQG = KC
        G_H = G_Q + NQG
        G_QH = G_H + GROUPS
        G_END = G_QH + 2 * GROUPS

        def act_groups(g):
            return sum(group_on_act(k) for k in range(g))

        def vec_groups(g):
            return g - act_groups(g)

        def wait_group_out(eng, g):
            if group_on_act(g):
                eng.wait_ge(turned_out_s, act_groups(g + 1))
            else:
                eng.wait_ge(turned_out_v, vec_groups(g + 1))

        def wait_groups_out(eng, g):
            if act_groups(g):
                eng.wait_ge(turned_out_s, act_groups(g))
            if vec_groups(g):
                eng.wait_ge(turned_out_v, vec_groups(g))

        EARLY = (0, 1, 2, 5, 6, 7)
        LATE = 2 * GROUPS - len(EARLY)
        LATE_AT = sorted([13 + 2 * k for k in range(LATE - GROUPS)] + [TILES - KC - GROUPS - 1 + k for k in range(GROUPS)])
        ALPHA_AT = [{TILES - KC + k: k for k in range(KC)}, {12 + 3 * k: k for k in range(KC)}]

        def late_groups(t):
            return len(EARLY) + sum(at < t for at in LATE_AT)

        def group_bank(g):
            if g < G_QH:
                return 4 + g % 4
            return EARLY[g - G_QH] if g - G_QH < len(EARLY) else TRA + g % 2

        UNITS = 2 * NP
        SPLIT_UNIT = UNITS - 3
        UNIT_AT = {t: (SPLIT_UNIT + 1 + i, k) for i in range(2) for k in range(KC) for t in [i * (KC + 1) + k]}

        def unit_on_act(u):
            return u % 2 == 1 or u >= SPLIT_UNIT

        def mix_bank(layer, j):
            return j + (5 if layer == 0 else 0)

        def unit_bank(u):
            return u % 4 if u < SPLIT_UNIT else TRA + 1 if u == SPLIT_UNIT else TRB

        def act_units(u):
            return sum(unit_on_act(k) for k in range(u))

        def wait_units_out(eng, u):
            eng.wait_ge(qg_out_v, u - act_units(u))
            if act_units(u):
                eng.wait_ge(qg_out_s, act_units(u))

        WgT_q, WgT_h, WqT_h, WqT_q = W[1], W[4], W[0], W[1]

        def group_dst(g):
            if g < G_Q:
                return WgT_q[:, g % KC, (g // KC) * HD:(g // KC + 1) * HD], HD
            if g < G_H:
                return qT[:, g - G_Q, :], NP * P
            if g < G_QH:
                k = g - G_H
                return WgT_h[:, k % KC, (k // KC) * HD:(k // KC + 1) * HD], HD
            k = (g - G_QH) % GROUPS
            dst = WqT_h if g - G_QH < GROUPS else WqT_q
            return dst[:, k % KC, (k // KC) * HD:(k // KC + 1) * HD], HD

        def copy_group(eng, g, done):
            dst, n = group_dst(g)
            eng.wait_ge(turned, g + 1)
            src = ps[:, group_bank(g), 0:n]
            ins = nc.vector.tensor_copy(dst, src) if done is turned_out_v else nc.scalar.copy(dst, src)
            ins.then_inc(done, 1)

        def wait_loaded(eng, key, part=0):
            eng.wait_ge(loaded[key][part], 16)

        def halves(dram):
            return dram.rearrange("(k p) n -> p k n", p=P)

        block = ctx.enter_context(nc.Block())

        @block.sync
        def _(sp):
            def load(key, dram, after=None, value=0):
                if after is not None:
                    sp.wait_ge(after, value)
                s = SLOT[key]
                n = KC // PARTS[key]
                v = halves(dram)
                for c in range(PARTS[key]):
                    sp.dma_start(W[s][:, c * n:(c + 1) * n, :], v[:, c * n:(c + 1) * n, :]).then_inc(loaded[key][c], 16)

            for i, name in enumerate(("src", "dst", "edge_type_3")):
                sp.dma_start(eidx[:, i, :], a[name].rearrange("(p c) -> p c", p=P)).then_inc(edges_loaded, 16)
            Wg, Wq = a["L0_gnn_Wg"], a["L0_gnn_Wq"]
            load("Wg_q", Wg[:, D:2 * D])
            for b in range(2):
                sp.dma_start(qn[b * L:(b + 1) * L, :, :],
                             a["L0_gnn_query_embs"].rearrange("(p b) l f -> b l p f", b=2)[b]).then_inc(q_loaded, 16)
            for i, name in enumerate(BIASES):
                sp.dma_start(bias[i:i + 1, :], a[name].rearrange("(o f) -> o f", o=1)).then_inc(bias_loaded, 16)
            load("Wg_h", Wg[:, 0:D])
            for h in range(2):
                sp.dma_start(xa[h * N:(h + 1) * N, :], a["x"][:, h * HD:(h + 1) * HD]).then_inc(x_loaded, 16)
            load("rel1_0", a["L0_gnn_W_rel1"][0])
            load("rel1_1", a["L0_gnn_W_rel1"][1])
            load("rel1_2", a["L0_gnn_W_rel1"][2], turned, GROUPS)
            load("root1", a["L0_gnn_W_root1"], turned, G_QH)
            load("Wq_h", Wq[:, 0:D], rgcn_done, 1)
            load("Wq_q", Wq[:, D:2 * D], rgcn_done, 2)
            load("rel2_0", a["L0_gnn_W_rel2"][0], rgcn_done, R + 1)
            load("rel2_1", a["L0_gnn_W_rel2"][1], qg_done, UNITS)
            load("rel2_2", a["L0_gnn_W_rel2"][2], turned, G_QH + GROUPS)
            load("root2", a["L0_gnn_W_root2"], turned, G_END)
            sp.wait_ge(qk_cleared, 1)
            for q, name in enumerate(("q", "k")):
                sp.dma_start(qk[:, :, 0, 4 * q:4 * q + 4], halves(a[f"L2_gnn_{name}1"]),
                             allow_slow_non_contiguous=True).then_inc(qk_loaded, 16)
                sp.dma_start(qk[:, :, 1, q:q + 1], halves(a[f"L2_gnn_{name}2"]),
                             allow_slow_non_contiguous=True).then_inc(qk_loaded, 16)
            done = R + 1
            load("L1_W", a["L1_gnn_W"], rgcn_done, done + 1)
            load("L2_W1_0", a["L2_gnn_W1"][0], rgcn_done, done + 2)
            load("L2_W1_1", a["L2_gnn_W1"][1], rgcn_done, done + 3)
            load("L2_W1_2", a["L2_gnn_W1"][2], rgcn_done, done + 4)
            load("L2_W2_0", a["L2_gnn_W2"][0], hg_done, 2)
            load("L2_W2_1", a["L2_gnn_W2"][1], alpha_done, 2)
            load("L2_W2_2", a["L2_gnn_W2"][2])
            load("L3_W1", a["L3_gnn_W1"], proj_done, 1)
            load("L3_W2", a["L3_gnn_W2"], rel_done, 3)
            sp.wait_ge(x_ready, 11)
            for h in range(2):
                sp.dma_start(out[:, h * HD:(h + 1) * HD], t0[h * N:(h + 1) * N, :]).then_inc(out_stored, 16)
            sp.wait_ge(out_stored, 32)

        @block.gpsimd
        def _(pool):
            made = [0]

            def link(ins):
                made[0] += 1
                ins.then_inc(pool_chain, 1)
                pool.wait_ge(pool_chain, made[0])

            link(nc.gpsimd.memset(ident[:, :], 0.0))
            nc.gpsimd.affine_select(out=ident[:, :], in_=ident[:, :], compare_op=ALU.not_equal, fill=1.0,
                                    base=0, pattern=[[-1, P]], channel_multiplier=1).then_inc(ident_ready, 1)
            link(nc.gpsimd.iota(cols_i, pattern=[[1, R * N]], base=0, channel_multiplier=0))
            nc.gpsimd.tensor_copy(cols_f, cols_i).then_inc(consts_ready, 1)
            nc.gpsimd.memset(small[:, 41:42], LN_EPS)
            pool.wait_ge(ident_ready, 1)
            nc.gpsimd.memset(blockd, 0.0).then_inc(consts_ready, 1)
            nc.gpsimd.tensor_copy(adjT[:, R, :], ident[:, :]).then_inc(consts_ready, 1)
            link(nc.gpsimd.tensor_tensor(avg[:, 0:N], ident[:, 0:N], ident[:, N:P], ALU.add))
            link(nc.gpsimd.tensor_scalar(avg[:, 0:N], avg[:, 0:N], 0.5, None, ALU.mult))
            link(nc.gpsimd.tensor_copy(avg[:, N:P], avg[:, 0:N]))
            link(nc.gpsimd.memset(rsel[:, :], 0.0))
            link(nc.gpsimd.memset(rsel[0:L, GN - 1:GN], 1.0))
            link(nc.gpsimd.memset(rsel[L:P, GN - 1 + NB:GN + NB], 1.0))
            link(nc.gpsimd.memset(i3[:, :], 0.0))
            for g in range(3):
                rows = i3[g * GN:(g + 1) * GN, :]
                link(nc.gpsimd.affine_select(out=rows, in_=rows, compare_op=ALU.not_equal, fill=1.0, base=0,
                                             pattern=[[-1, GN]], channel_multiplier=1))
            for g in range(PPG):
                rows = i3[:, g * 2 * NB:(g + 1) * 2 * NB].rearrange("p (b n) -> p n b", b=2)
                nc.gpsimd.tensor_copy(bsel[:, g * NB:(g + 1) * NB, :].rearrange("p n (b l) -> p n b l", b=2),
                                      rows.unsqueeze(3).to_broadcast([3 * GN, NB, 2, L])).then_inc(consts_ready, 1)

            nc.gpsimd.memset(qk[:, :, :, :], 0.0).then_inc(qk_cleared, 1)
            link(nc.gpsimd.tensor_tensor(qsel[:, :], ident[:, 0:GN], ident[:, GN:2 * GN], ALU.add))
            for g in range(2, P // GN):
                link(nc.gpsimd.tensor_tensor(qsel[:, :], qsel[:, :], ident[:, g * GN:(g + 1) * GN], ALU.add))
            nb = len(BIASES)
            link(nc.gpsimd.memset(biases[:, :], 0.0))
            pool.wait_ge(bias_loaded, 16 * nb)
            link(nc.gpsimd.tensor_copy(biases[0:nb, :], bias[:, :]))
            link(nc.gpsimd.tensor_tensor(bias[:, :], bias[:, :], biases[0:nb, :], ALU.subtract))
            link(nc.gpsimd.tensor_copy(bias_mid[:, :], bias[:, :]))
            link(nc.gpsimd.tensor_tensor(bias[:, :], bias[:, :], bias_mid[:, :], ALU.subtract))
            nc.gpsimd.tensor_copy(biases[GN:GN + nb, :], bias_mid[:, :]).then_inc(biases_split, 1)
            nc.gpsimd.tensor_copy(biases[2 * GN:2 * GN + nb, :], bias[:, :]).then_inc(biases_split, 1)

            for layer in range(2):
                for t in range(TILES):
                    T = layer * TILES + t
                    if not on_pool(T):
                        continue
                    pool.wait_ge(sig_ready, T + 1)
                    if T >= PRODS:
                        pool.wait_ge(reduced, T - PRODS + 1)
                    nc.gpsimd.tensor_tensor(prod[:, T % PRODS, :], pre[:, T % PRES, :],
                                            qn[:, t // NB, :], ALU.mult).then_inc(prod_p, 1)

        @block.scalar
        def _(act):
            made = [0]

            def link(ins):
                made[0] += 1
                ins.then_inc(act_chain, 1)
                act.wait_ge(act_chain, made[0])

            for g in range(G_H):
                if group_on_act(g):
                    copy_group(act, g, turned_out_s)
            act.wait_ge(deg_ready, 1)
            nc.scalar.activation(small[:, 9:10], small[:, 8:9], ACT.Sqrt).then_inc(sqrt_deg, 1)
            act.wait_ge(sqrt_deg, 1)
            nc.scalar.activation(small[:, 42:43], small[:, 9:10], ACT.Sigmoid)

            def unit_copy(u):
                act.wait_ge(qg_done, u + 1)
                nc.scalar.copy(qg[:, u // 2, (u % 2) * HD:(u % 2 + 1) * HD], ps[:, unit_bank(u), 0:HD]).then_inc(qg_out_s, 1)

            unit_copy(1)
            for g in range(G_H, G_QH):
                if group_on_act(g):
                    copy_group(act, g, turned_out_s)
            for u in range(3, SPLIT_UNIT, 2):
                unit_copy(u)

            def mix_copy(layer):
                act.wait_ge(mixed, 3 * layer + 2)
                nc.scalar.copy(mixT[:, 1, :], ps[:, mix_bank(layer, 1), :]).then_inc(mix_out_s, 1)

            for layer in range(2):
                mix_copy(layer)
                if layer == 0:
                    for k in range(len(EARLY)):
                        copy_group(act, G_QH + k, turned_out_s)
                def stack_part(i, g, h):
                    part, stacked = ((hi, hi_stacked), (mid, mid_stacked))[i]
                    nc.scalar.copy(stack[i * GN:(i + 1) * GN, h, g, :],
                                   part[h * N + g * GN:h * N + (g + 1) * GN, :]).then_inc(stacked, 1)

                for i, ready in enumerate((hi_ready, mid_ready)):
                    act.wait_ge(ready, layer + 1)
                    for h in range(2):
                        stack_part(i, 0, h)
                if layer == 0:
                    unit_copy(SPLIT_UNIT)
                    act.wait_ge(qg_out_s, act_units(SPLIT_UNIT + 1))
                for t in range(TILES):
                    T = layer * TILES + t
                    if layer == 0:
                        for k in range(late_groups(t + 1) if t else len(EARLY), late_groups(t + 2)):
                            copy_group(act, G_QH + k, turned_out_s)
                    if layer == 0 and UNIT_AT.get(t, (0, 0))[1] == KC - 1:
                        unit_copy(UNIT_AT[t][0])
                    if T in TENSOR_ADDS:
                        act.wait_ge(hg_cast, T + 1)
                        if on_pool(T - PRES):
                            act.wait_ge(prod_p, pool_tiles(T - PRES + 1))
                        else:
                            act.wait_ge(prod_v, vec_tiles(T - PRES + 1))
                    else:
                        act.wait_ge(pre_ready, vec_adds(T + 1))
                    if 2 <= t < 6:
                        stack_part((t - 2) // 2, 1, t % 2)
                    src = ring(T) if T in TENSOR_ADDS else by_half(pre[:, T % PRES, :])
                    nc.scalar.activation(by_half(pre[:, T % PRES, :]), src, ACT.Sigmoid).then_inc(sig_ready, 1)
                act.wait_ge(reduced, (layer + 1) * TILES)
                for q in range(2, 4):
                    for g in range(N // GN):
                        nc.scalar.copy(t0[N + g * GN:N + (g + 1) * GN, (q % 2) * QW:(q % 2 + 1) * QW],
                                       ps[q * GN:(q + 1) * GN, ACC, g * QW:(g + 1) * QW]).then_inc(qi_out_s, 1)
                act.wait_ge(qi_out_v, 4 * (layer + 1))
                act.wait_ge(qi_out_s, 4 * (layer + 1))
                nc.scalar.activation(t2[:, :], t0[:, :], ACT.Tanh).then_inc(tanh_ready, 1)
                act.wait_ge(alpha_done, layer + 1)
                nc.scalar.activation(t1[:, :], ps[:, TRB, 0:HD], ACT.Sigmoid).then_inc(alpha_ready, 1)

            def ln(n):
                act.wait_ge(ln_var, n)
                nc.scalar.activation(small[:, 5:6], small[:, 4:5], ACT.Sqrt, bias=small[:, 41:42]).then_inc(ln_std, 1)

            ln(1)
            ln(2)
            for layer in range(2):
                hp = 2 - layer
                act.wait_ge(rel_done, 3 * layer + 1)
                nc.scalar.copy(X2[:, HD:D], ps[N:P, 2, 0:HD]).then_inc(X_out_s, 1)
                act.wait_ge(rel_done, 3 * layer + 3)
                nc.scalar.copy(X01[:, HD:D], ps[:, 1, 0:HD]).then_inc(X_out_s, 1)
                act.wait_ge(X_turned, 3 * layer + 3)
                nc.scalar.copy(XT[:, JC:KC, 0:P], ps[:, 4, 0:HD].rearrange("p (k n) -> p k n", k=JC)).then_inc(XT_out_s, 1)
                act.wait_ge(shifted, layer + 1)
                n = R * N
                for h in range(hp):
                    nc.scalar.activation(expd[:, h * n:(h + 1) * n], leaky[:, h * n:(h + 1) * n], ACT.Exp,
                                         bias=small[:, 16 + h:17 + h]).then_inc(exp_ready, 1)
                act.wait_ge(wts_turned, layer + 1)
                nc.scalar.copy(wT2[:, 0:hp * P], ps[0:N, 7, 0:hp * P]).then_inc(wT_out_s, 1)
                if layer == 0:
                    act.wait_ge(elu_min, 1)
                    nc.scalar.activation(t2[:, :], t2[:, :], ACT.Exp).then_inc(elu_exp, 1)
            ln(3)
            ln(4)

        @block.vector
        def _(dve):
            made = [0]

            def link(ins):
                made[0] += 1
                ins.then_inc(vec_chain, 1)
                dve.wait_ge(vec_chain, made[0])

            dve.wait_ge(edges_loaded, 48)
            link(nc.vector.tensor_copy(edge_f, eidx[:, :, :]))
            link(nc.vector.scalar_tensor_tensor(out=edge_f[:, 0, :], in0=edge_f[:, 2, :], scalar=float(N),
                                                in1=edge_f[:, 0, :], op0=ALU.mult, op1=ALU.add))
            dve.wait_ge(consts_ready, 1)
            nc.vector.tensor_tensor(hot_src, cols_f.unsqueeze(1).to_broadcast([P, EC, R * N]),
                                    edge_f[:, 0, :].unsqueeze(2).to_broadcast([P, EC, R * N]),
                                    ALU.is_equal).then_inc(hot_ready, 1)
            for h in range(2):
                nc.vector.tensor_tensor(hot_dst[:, :, h * N:(h + 1) * N], cols_f[:, 0:N].unsqueeze(1).to_broadcast([P, EC, N]),
                                        edge_f[:, 1, :].unsqueeze(2).to_broadcast([P, EC, N]),
                                        ALU.is_equal).then_inc(hot_ready, 1)
            def copy_groups(gs):
                for g in gs:
                    if not group_on_act(g):
                        copy_group(dve, g, turned_out_v)

            dve.wait_ge(counts_done, 1)
            link(nc.vector.tensor_copy(M[:, :], ps[:, 0, 0:R * N]))
            copy_groups(range(G_H))
            link(nc.vector.tensor_scalar(maskb[:, :], M[:, :], 0.0, NEG, ALU.is_equal, ALU.mult))
            link(nc.vector.tensor_reduce(small[:, 0:R], M[:, :].rearrange("p (r n) -> p r n", r=R), AX.X, ALU.add))
            link(nc.vector.tensor_reduce(small[:, 7:8], small[:, 0:R], AX.X, ALU.add))
            nc.vector.tensor_scalar(small[:, 8:9], small[:, 7:8], 1.0, None, ALU.add).then_inc(deg_ready, 1)
            link(nc.vector.tensor_scalar(small[:, 0:R], small[:, 0:R], 1.0, None, ALU.max))
            link(nc.vector.reciprocal(small[:, 10:10 + R], small[:, 0:R]))
            dve.wait_ge(consts_ready, 3)
            for h in range(2):
                rows = slice(h * N, (h + 1) * N)
                m3 = M[rows, :].rearrange("p (r n) -> p r n", r=R)
                link(nc.vector.tensor_tensor(blockd[rows, 0:R, rows], m3,
                                             small[rows, 10:10 + R].unsqueeze(2).to_broadcast([N, R, N]), ALU.mult))
                link(nc.vector.tensor_reduce(blockd[rows, R, rows], M[rows, :].rearrange("p (r n) -> p n r", r=R),
                                             AX.X, ALU.add))
            link(nc.vector.tensor_tensor(blockd[:, R, :], blockd[:, R, :], ident[:, :], ALU.add))
            dve.wait_ge(sqrt_deg, 1)
            link(nc.vector.reciprocal(small[:, 13:14], small[:, 9:10]))
            nc.vector.tensor_scalar(blockd[:, R, :], blockd[:, R, :], small[:, 13:14], None, ALU.mult).then_inc(blocks_ready, 1)
            def unit_copy(u):
                dve.wait_ge(qg_done, u + 1)
                nc.vector.tensor_copy(qg[:, u // 2, 0:HD], ps[:, unit_bank(u), 0:HD]).then_inc(qg_out_v, 1)

            unit_copy(0)
            copy_groups(range(G_H, G_QH))
            dve.wait_ge(adj_turned, 1)
            nc.vector.tensor_copy(adjT[:, 0:R, :], ps[:, TRA, 0:R * P].rearrange("p (r n) -> p r n", r=R)).then_inc(adj_ready, 1)
            nc.vector.tensor_scalar(gcnT[:, :], ps[:, TRA, R * P:(R + 1) * P], small[:, 13:14], None, ALU.mult).then_inc(adj_ready, 1)
            for u in range(2, SPLIT_UNIT - 1, 2):
                unit_copy(u)

            def blocks_out(dst, turned_, ready, n):
                dve.wait_ge(turned_, 2 * n - 1)
                nc.vector.tensor_copy(dst[:, 0, :], ps[:, NODE_BANKS[0], 0:P]).then_inc(ready, 1)
                dve.wait_ge(turned_, 2 * n)
                nc.vector.tensor_copy(dst[:, 1:JC, :], ps[:, NODE_BANKS[1], 0:HD - P].rearrange("p (j n) -> p j n", j=JC - 1)).then_inc(ready, 1)

            def layer_norm(y, dst, n):
                link(nc.vector.bn_stats(small[:, 20:26], y))
                nc.vector.bn_aggr(small[:, 0:2], small[:, 20:26]).then_inc(ln_parts, 1)
                dve.wait_ge(ln_mean, n)
                dve.wait_ge(ln_parts, n)
                link(nc.vector.tensor_tensor(small[:, 6:7], small[:, 0:1], ps[:, TRB, 0:1], ALU.subtract))
                nc.vector.scalar_tensor_tensor(out=small[:, 4:5], in0=small[:, 6:7], scalar=small[:, 6:7],
                                               in1=ps[:, TRB, 1:2], op0=ALU.mult, op1=ALU.add).then_inc(ln_var, 1)
                link(nc.vector.tensor_copy(small[:, 2:3], ps[:, TRB, 0:1]))
                dve.wait_ge(ln_std, n)
                link(nc.vector.reciprocal(small[:, 6:7], small[:, 5:6]))
                for cols in (BLOCKS if n < 4 else (slice(0, HD),)):
                    nc.vector.tensor_scalar(dst[:, cols], y[:, cols], small[:, 2:3], small[:, 6:7],
                                            ALU.subtract, ALU.mult).then_inc(x_ready, 1)

            for layer in range(2):
                for i, j in enumerate((0, 2)):
                    dve.wait_ge(mixed, 3 * layer + j + 1)
                    nc.vector.tensor_copy(mixT[:, j, :], ps[:, mix_bank(layer, j), :]).then_inc(mix_out_v, 1)
                if layer == 0:
                    unit_copy(SPLIT_UNIT - 1)
                dve.wait_ge(rgcn_done, (R + 1) * (layer + 1))
                for cols in BLOCKS:
                    nc.vector.tensor_scalar(hh[:, cols], ps[:, ACC, cols], 0.0, None, ALU.max).then_inc(h_ready, 1)
                if layer == 0:
                    dve.wait_ge(node_turned, 2)
                    nc.vector.tensor_copy(nodeT[:, :, :], ps[:, NODE_BANKS[0], 0:HD].rearrange("p (j n) -> p j n", j=JC)).then_inc(nodeT_ready, 2)
                else:
                    blocks_out(nodeT, node_turned, nodeT_ready, 2)
                dve.wait_ge(hg_done, layer + 1)
                nc.vector.tensor_copy(hi[:, :], ps[:, HG[layer], 0:HD]).then_inc(hi_ready, 1)
                dve.wait_ge(hi_ready, layer + 1)
                link(nc.vector.tensor_tensor(t1[:, :], ps[:, HG[layer], 0:HD], hi[:, :], ALU.subtract))
                nc.vector.tensor_copy(mid[:, :], t1[:, :]).then_inc(mid_ready, 1)
                dve.wait_ge(mid_ready, layer + 1)

                def stack_low(g, h):
                    r = slice(h * N + g * GN, h * N + (g + 1) * GN)
                    nc.vector.tensor_tensor(stack[2 * GN:3 * GN, h, g, :], t1[r, :], mid[r, :],
                                            ALU.subtract).then_inc(lo_stacked, 1)

                for h in range(2):
                    stack_low(0, h)
                LAG = 2
                for t in range(TILES + LAG):
                    T = layer * TILES + t
                    if 2 <= t < 4:
                        stack_low(1, t % 2)
                    if layer == 0 and t % NB == 0 and t < TILES:
                        wait_units_out(dve, 2 * (t // NB + 1))
                    if t < TILES and T not in TENSOR_ADDS:
                        dve.wait_ge(hg_cast, T + 1)
                        if T >= PRES:
                            if on_pool(T - PRES):
                                dve.wait_ge(prod_p, pool_tiles(T - PRES + 1))
                            else:
                                dve.wait_ge(prod_v, vec_tiles(T - PRES + 1))
                        nc.vector.tensor_tensor(by_half(pre[:, T % PRES, :]), ring(T), by_half(qg[:, t // NB, :]),
                                                ALU.add).then_inc(pre_ready, 1)
                    if t >= LAG and not on_pool(T - LAG):
                        T -= LAG
                        dve.wait_ge(sig_ready, T + 1)
                        if T >= PRODS:
                            dve.wait_ge(reduced, T - PRODS + 1)
                        nc.vector.tensor_tensor(prod[:, T % PRODS, :], pre[:, T % PRES, :],
                                                qn[:, (t - LAG) // NB, :], ALU.mult).then_inc(prod_v, 1)
                dve.wait_ge(reduced, (layer + 1) * TILES)
                for q in range(2):
                    for g in range(N // GN):
                        nc.vector.tensor_copy(t0[g * GN:(g + 1) * GN, q * QW:(q + 1) * QW],
                                              ps[q * GN:(q + 1) * GN, ACC, g * QW:(g + 1) * QW]).then_inc(qi_out_v, 1)
                blocks_out(qiT, qi_turned, qiT_ready, layer + 1)
                dve.wait_ge(tanh_ready, layer + 1)
                link(nc.vector.tensor_tensor(t2[:, :], t2[:, :], hh[:, :], ALU.subtract))
                if layer == 1:
                    link(nc.vector.tensor_tensor(hh[:, :], hh[:, :], xa[:, :], ALU.add))
                dve.wait_ge(alpha_ready, layer + 1)
                link(nc.vector.tensor_tensor(t1[:, :], t1[:, :], t2[:, :], ALU.mult))
                if layer == 0:
                    for cols in BLOCKS:
                        nc.vector.tensor_tensor(hx[:, cols], t1[:, cols], hh[:, cols], ALU.add).then_inc(x_ready, 1)
                else:
                    link(nc.vector.tensor_tensor(t0[:, :], t1[:, :], hh[:, :], ALU.add))
            layer_norm(t0[:, :], xa[:, :], 1)

            blocks_out(nodeT, node_turned, nodeT_ready, 3)
            dve.wait_ge(proj_done, 1)
            layer_norm(ps[:, ACC, 0:HD], xa[:, :], 2)

            for layer in range(2):
                hp = 2 - layer
                bw = HD // hp
                n = R * N
                blocks_out(nodeT, node_turned, nodeT_ready, 4 + layer)
                dve.wait_ge(rel_done, 3 * layer + 1)
                nc.vector.tensor_copy(X2[:, 0:HD], ps[0:N, 2, 0:HD]).then_inc(X_out_v, 1)
                dve.wait_ge(X_turned, 3 * layer + 1)
                nc.vector.tensor_copy(XT[:, :, P:n], ps[:, 5, 0:HD].rearrange("p (k n) -> p k n", k=KC)).then_inc(XT_out_v, 1)
                dve.wait_ge(rel_done, 3 * layer + 2)
                nc.vector.tensor_copy(X01[:, 0:HD], ps[:, 0, 0:HD]).then_inc(X_out_v, 1)
                dve.wait_ge(X_turned, 3 * layer + 2)
                nc.vector.tensor_copy(XT[:, 0:JC, 0:P], ps[:, 3, 0:HD].rearrange("p (k n) -> p k n", k=JC)).then_inc(XT_out_v, 1)
                dve.wait_ge(qk_done, layer + 1)
                nc.vector.tensor_copy(QKT, ps[:, ACC, 0:n]).then_inc(qkT_ready, 1)
                dve.wait_ge(score_done, layer + 1)
                link(nc.vector.tensor_copy(score[:, 0:hp * n], ps[:, 0, 0:hp * n]))
                link(nc.vector.scalar_tensor_tensor(out=leaky[:, 0:hp * n], in0=score[:, 0:hp * n], scalar=SLOPE,
                                                    in1=score[:, 0:hp * n], op0=ALU.mult, op1=ALU.max))
                nc.vector.tensor_reduce(small[:, 16:16 + hp], leaky[:, 0:hp * n].rearrange("p (h c) -> p h c", h=hp),
                                        AX.X, ALU.max, negate=True).then_inc(shifted, 1)
                for h in range(hp):
                    dve.wait_ge(exp_ready, 2 * layer + h + 1)
                    nc.vector.tensor_tensor_reduce(wts[:, h * n:(h + 1) * n], expd[:, h * n:(h + 1) * n], M[:, :], 1.0, 0.0,
                                                   ALU.mult, ALU.add, small[:, 18 + h:19 + h]).then_inc(wts_ready, 1)
                dve.wait_ge(wts_turned, layer + 1)
                nc.vector.tensor_copy(wT1[:, 0:hp * P], ps[:, 3, 0:hp * P]).then_inc(wT_out_v, 1)
                link(nc.vector.tensor_scalar(small[:, 18:18 + hp], small[:, 18:18 + hp], SOFTMAX_EPS, None, ALU.add))
                link(nc.vector.reciprocal(small[:, 32:32 + hp], small[:, 18:18 + hp]))
                dve.wait_ge(addend_done, layer + 1)
                link(nc.vector.tensor_copy(t1[:, :], ps[:, ADDEND, 0:HD]))
                dve.wait_ge(att_done, layer + 1)
                for h in range(hp):
                    ins = nc.vector.scalar_tensor_tensor(out=t0[:, h * bw:(h + 1) * bw], in0=ps[:, ACC, h * bw:(h + 1) * bw],
                                                         scalar=small[:, 32 + h:33 + h], in1=t1[:, h * bw:(h + 1) * bw],
                                                         op0=ALU.mult, op1=ALU.add)
                link(ins)
                if layer == 0:
                    nc.vector.tensor_scalar(t2[:, :], t0[:, :], 0.0, None, ALU.min).then_inc(elu_min, 1)
                    link(nc.vector.tensor_scalar(t0[:, :], t0[:, :], 0.0, None, ALU.max))
                    dve.wait_ge(elu_exp, 1)
                    for cols in BLOCKS:
                        nc.vector.scalar_tensor_tensor(out=hx[:, cols], in0=t2[:, cols], scalar=-1.0, in1=t0[:, cols],
                                                       op0=ALU.add, op1=ALU.add).then_inc(x_ready, 1)
                else:
                    layer_norm(t0[:, :], xa[:, :], 3)
            blocks_out(nodeT, node_turned, nodeT_ready, 6)
            dve.wait_ge(proj_done, 2)
            for cols in BLOCKS:
                nc.vector.tensor_scalar(hx[:, cols], ps[:, ACC, cols], 0.0, None, ALU.max).then_inc(y_ready, 1)
            blocks_out(nodeT, node_turned, nodeT_ready, 7)
            dve.wait_ge(proj_done, 3)
            layer_norm(ps[:, LAST, 0:HD], t0[:, :], 4)

        @block.tensor
        def _(pe):
            def turn_blocks(g, blocks):
                at = 0
                for src in blocks:
                    ins = nc.tensor.transpose(ps[:, group_bank(g), at:at + P], src, ident[:, :])
                    at += P
                ins.then_inc(turned, 1)

            def turn_weight(g0, key, k):
                part, col = k // KC, k % KC
                if col == 0:
                    wait_loaded(pe, key, part)
                if g0 < G_QH:
                    if g0 + k >= 4:
                        wait_group_out(pe, g0 + k - 4)
                elif g0 + k >= G_QH + len(EARLY):
                    wait_group_out(pe, g0 + k - 2)
                src = W[SLOT[key]]
                turn_blocks(g0 + k, [src[:, part * JC + i, col * P:(col + 1) * P] for i in range(JC)])

            BY_BLOCK = [h * JC + j for j in range(JC) for h in range(2)]

            def project(T, w, bank, first=True, last=True, col0=0, chunks=BY_BLOCK, waits={}):
                for i, k in enumerate(chunks):
                    h, j = k // JC, k % JC
                    if i in waits:
                        pe.wait_ge(*waits[i])
                    for c in range(2):
                        ins = nc.tensor.matmul(ps[c * N:(c + 1) * N, bank, 0:HD],
                                               T[:, j, col0 + h * N:col0 + (h + 1) * N],
                                               w[:, k, c * HD:(c + 1) * HD],
                                               start=(first and k == 0), stop=(last and k == chunks[-1]),
                                               skip_group_check=True)
                return ins

            def add_nodes(x, bank):
                for c in range(2):
                    ins = nc.tensor.matmul(ps[c * N:(c + 1) * N, bank, 0:HD], ident[:, c * N:(c + 1) * N],
                                           x[:, :], start=False, stop=False, skip_group_check=True)
                return ins

            def add_bias(name, bank):
                i = BIASES.index(name)
                for c in range(2):
                    ins = nc.tensor.matmul(ps[c * N:(c + 1) * N, bank, 0:HD],
                                           i3[:, i:i + 1].to_broadcast([3 * GN, N]),
                                           biases[:, c * HD:(c + 1) * HD], start=True, stop=False, skip_group_check=True)
                return ins

            def wait_block(made, j):
                if made is not None and j < 2:
                    pe.wait_ge(made[0], 2 * made[1] - 1 + j)

            def turn_nodes(y, right, done, banks=NODE_BANKS, made=None):
                for j in range(JC):
                    wait_block(made, j)
                    at = j * P if len(banks) == 1 else max(j - 1, 0) * P
                    out_j = ps[:, banks[min(j, len(banks) - 1)], at:at + P]
                    if right is ident:
                        ins = nc.tensor.transpose(out_j, y[:, j * P:(j + 1) * P], ident[:, :])
                    else:
                        ins = nc.tensor.matmul(out_j, y[:, j * P:(j + 1) * P], right[:, :], start=True, stop=True)
                    if j == JC - 1:
                        ins.then_inc(done, 3 - len(banks))
                    elif j == 0 and len(banks) == 2:
                        ins.then_inc(done, 1)

            def as_copied(ready, n):
                return {0: (ready, 2 * n - 1), 2: (ready, 2 * n)}

            def keep_warm(n, bank):
                for _ in range(n):
                    nc.tensor.matmul(ps[:, bank, :], bsel[:, 0, :], bsel[:, 0:4, :].rearrange("p a b -> p (a b)"),
                                     start=True, stop=True, skip_group_check=True)

            pe.wait_ge(hot_ready, 3)
            for c in range(EC):
                ins = nc.tensor.matmul(ps[:, 0, 0:R * N], hot_dst[:, c, :], hot_src[:, c, :],
                                       start=(c == 0), stop=(c == EC - 1))
            ins.then_inc(counts_done, 1)
            pe.wait_ge(ident_ready, 1)
            for k in range(GROUPS):
                turn_weight(0, "Wg_q", k)
            pe.wait_ge(q_loaded, 32)
            for k in range(NQG):
                wait_group_out(pe, G_Q + k - 4)
                turn_blocks(G_Q + k, [qn[:, p, k * P:(k + 1) * P] for p in range(NP)])
            def query_unit(u, chunks=range(KC)):
                if 4 <= u < SPLIT_UNIT:
                    wait_units_out(pe, u - 3)
                if u == UNITS - 1 and chunks[0] == 0:
                    wait_units_out(pe, u)
                p, c = u // 2, u % 2
                for k in chunks:
                    ins = nc.tensor.matmul(ps[:, unit_bank(u), 0:HD], qT[:, k, p * P:(p + 1) * P],
                                           WgT_q[:, k, c * HD:(c + 1) * HD], start=(k == 0), stop=(k == KC - 1))
                if k == KC - 1:
                    ins.then_inc(qg_done, 1)

            def turn_wq(ks):
                for k in ks:
                    turn_weight(G_QH + (k // GROUPS) * GROUPS, ("Wq_h", "Wq_q")[k // GROUPS], k % GROUPS)

            def mix(layer, x):
                for j in range(JC):
                    if layer == 1:
                        wait_block((x_ready, 1), j)
                    nc.tensor.matmul(ps[:, mix_bank(layer, j), :], x[:, j * P:(j + 1) * P],
                                     adjT[:, :, :].rearrange("p r n -> p (r n)"),
                                     start=True, stop=True).then_inc(mixed, 1)

            for u in range(SPLIT_UNIT):
                if u == 0:
                    wait_groups_out(pe, G_H)
                if u == 2:
                    for k in range(GROUPS):
                        turn_weight(G_H, "Wg_h", k)
                    wait_groups_out(pe, G_QH)
                    pe.wait_ge(blocks_ready, 1)
                    for r in range(R + 1):
                        ins = nc.tensor.transpose(ps[:, TRA, r * P:(r + 1) * P], blockd[:, r, :], ident[:, :])
                    ins.then_inc(adj_turned, 1)
                if u == SPLIT_UNIT - 1:
                    pe.wait_ge(x_loaded, 32)
                    pe.wait_ge(adj_ready, 2)
                    mix(0, xa)
                query_unit(u)

            def copy_queries(T, c):
                nc.tensor.matmul(ring(T)[:, c, :], ident[:, :], qg[:, T % TILES // NB, c * HD:(c + 1) * HD],
                                 start=True, stop=False)

            def gate(layer):
                if layer == 0:
                    pe.wait_ge(consts_ready, 5)
                LAG = 5
                for t in range(TILES + LAG):
                    T = layer * TILES + t
                    if t % (PPG * NB) == 0 and t < TILES:
                        g = t // (PPG * NB)
                        pe.wait_ge(hi_stacked, 4 * layer + 2 * (g + 1))
                        pe.wait_ge(mid_stacked, 4 * layer + 2 * (g + 1))
                        pe.wait_ge(lo_stacked, 4 * layer + 2 * (g + 1))
                    if t <= TILES:
                        before = T - RING[layer]
                        if before in TENSOR_ADDS:
                            pe.wait_ge(sig_ready, before + 1)
                        elif t >= RING[layer]:
                            pe.wait_ge(pre_ready, vec_adds(before + 1))
                    if TILES <= t < TILES + LAG - 1:
                        keep_warm(1, TRA)
                    if t < TILES:
                        p, n = t // NB, t % NB
                        for c in range(2):
                            if T in TENSOR_ADDS and T not in AHEAD:
                                copy_queries(T, c)
                            ins = nc.tensor.matmul(ring(T)[:, c, :], bsel[:, (p % PPG) * NB + n, :],
                                                   stack[:, c, p // PPG, :], start=T not in TENSOR_ADDS, stop=True)
                        ins.then_inc(hg_cast, 1)
                    if layer == 1 and t < 8:
                        keep_warm(1, TRB)
                    if layer == 0 and t in UNIT_AT:
                        query_unit(UNIT_AT[t][0], [UNIT_AT[t][1]])
                    if layer == 0 and t < TILES:
                        if t == LATE_AT[0]:
                            wait_units_out(pe, SPLIT_UNIT + 1)
                        turn_wq(range(late_groups(t), late_groups(t + 1)))
                    if t in ALPHA_AT[layer]:
                        if layer == 0 and ALPHA_AT[layer][t] == 0:
                            wait_groups_out(pe, G_END)
                        if ALPHA_AT[layer][t] == 0:
                            if layer == 0:
                                wait_units_out(pe, UNITS)
                            add_bias("L0_gnn_bq", TRB)
                        project(nodeT, WqT_h, TRB, first=False, last=False, chunks=[ALPHA_AT[layer][t]])
                    if t >= LAG:
                        T -= LAG
                        if on_pool(T):
                            pe.wait_ge(prod_p, pool_tiles(T + 1))
                        else:
                            pe.wait_ge(prod_v, vec_tiles(T + 1))
                        p, n = (t - LAG) // NB, (t - LAG) % NB
                        g, s = p // PPG, GN - 1 - (p % PPG) * 2 * NB - n
                        for q in range(4):
                            ins = nc.tensor.matmul(ps[q * GN:(q + 1) * GN, ACC, g * QW:(g + 1) * QW], rsel[:, s:s + GN],
                                                   prod[:, T % PRODS, q * QW:(q + 1) * QW],
                                                   start=(t == LAG), stop=(t == TILES + LAG - 1), skip_group_check=True)
                        ins.then_inc(reduced, 1)

            for layer in range(2):
                if layer == 1:
                    mix(1, hx)
                if layer == 0:
                    pe.wait_ge(mix_out_v, 2)
                    pe.wait_ge(mix_out_s, 1)
                    pe.wait_ge(biases_split, 2)
                add_bias(f"L0_gnn_b{layer + 1}", ACC)
                for r in range(R + 1):
                    key = f"rel{layer + 1}_{r}" if r < R else f"root{layer + 1}"
                    wait_loaded(pe, key)
                    waits = {0: (mix_out_v, 3), 2: (mix_out_s, 2), 4: (mix_out_v, 4)} if (layer, r) == (1, 0) else {}
                    project(mixT, W[SLOT[key]], ACC, first=False, last=(r == R),
                            col0=r * P, waits=waits).then_inc(rgcn_done, 1)
                if layer == 0:
                    wait_units_out(pe, SPLIT_UNIT)
                    turn_wq(range(0, 3))
                turn_nodes(hh, ident, node_turned, NODE_BANKS[:layer + 1], made=(h_ready, layer + 1))
                if layer == 0:
                    turn_wq(range(3, len(EARLY)))
                add_bias("L0_gnn_bg", HG[layer])
                project(nodeT, WgT_h, HG[layer], first=False, waits=as_copied(nodeT_ready, layer + 1)).then_inc(hg_done, 1)
                if layer == 1:
                    for T in AHEAD:
                        for c in range(2):
                            copy_queries(T, c)
                if layer == 0:
                    wait_groups_out(pe, G_QH + len(EARLY))
                    query_unit(SPLIT_UNIT)
                gate(layer)
                keep_warm(1, 2)
                pe.wait_ge(qi_out_v, 4 * (layer + 1))
                pe.wait_ge(qi_out_s, 4 * (layer + 1))
                turn_nodes(t0, ident, qi_turned)
                keep_warm(1, 2)
                project(qiT, WqT_q, TRB, first=False, waits=as_copied(qiT_ready, layer + 1)).then_inc(alpha_done, 1)
                keep_warm(6 if layer == 0 else 12, 4)

            def norm_stats(n, name=None):
                if n > 1:
                    keep_warm(5, 4)
                pe.wait_ge(ln_parts, n)
                nc.tensor.matmul(ps[:, TRB, 0:2], avg[:, :], small[:, 0:2], start=True, stop=True).then_inc(ln_mean, 1)
                if name is not None:
                    add_bias(name, ACC)
                keep_warm(4, 4)

            def gcn(n, key, x, made, bank, residual=None):
                turn_nodes(x, gcnT, node_turned, made=made)
                if residual is not None:
                    add_nodes(residual, bank)
                else:
                    keep_warm(1, 4)
                wait_loaded(pe, key)
                project(nodeT, W[SLOT[key]], bank, first=False, waits=as_copied(nodeT_ready, n)).then_inc(proj_done, 1)

            norm_stats(1, "L1_gnn_b")
            gcn(3, "L1_W", xa, (x_ready, 2), ACC, xa)
            norm_stats(2)

            pe.wait_ge(qk_loaded, 64)
            for layer in range(2):
                hp = 2 - layer
                bw = HD // hp
                m = 4 * hp if hp == 2 else 2
                n = R * N
                x = xa if layer == 0 else hx
                turn_nodes(x, ident, node_turned, made=(x_ready, 3 + layer))
                keep_warm(1, 4)
                keys = [f"L2_W{layer + 1}_{r}" for r in range(R)]
                wait_loaded(pe, keys[2])
                project(nodeT, W[SLOT[keys[2]]], 2, waits=as_copied(nodeT_ready, 4 + layer)).then_inc(rel_done, 1)
                wait_loaded(pe, keys[0])
                wait_loaded(pe, keys[1])
                def turn_pair(c):
                    pe.wait_ge((X_out_v, X_out_s)[c], 2 * layer + 2)
                    for i in range(JC):
                        ins = nc.tensor.transpose(ps[:, 3 + c, i * P:(i + 1) * P], X01[:, (c * JC + i) * P:(c * JC + i + 1) * P],
                                                  ident[:, :])
                    ins.then_inc(X_turned, 1)

                def times_qk(k, cols):
                    g = k % (P // GN)
                    return nc.tensor.matmul(ps[g * GN:(g + 1) * GN, ACC, cols], qk[:, k, layer, :], XT[:, k, cols],
                                            start=(k == g and cols == OTHER), stop=(k + P // GN >= KC), skip_group_check=True)

                PAIR, OTHER = slice(0, P), slice(P, n)
                for c in range(2):
                    for i, k in enumerate(BY_BLOCK):
                        h, j = k // JC, k % JC
                        for r in range(2):
                            ins = nc.tensor.matmul(ps[r * N:(r + 1) * N, c, 0:HD], nodeT[:, j, h * N:(h + 1) * N],
                                                   W[SLOT[keys[r]]][:, k, c * HD:(c + 1) * HD],
                                                   start=(i == 0), stop=(i == KC - 1), skip_group_check=True)
                        if c == 0 and i == 2:
                            pe.wait_ge(X_out_v, 2 * layer + 1)
                            pe.wait_ge(X_out_s, 2 * layer + 1)
                            for b in range(KC):
                                turn = nc.tensor.transpose(ps[:, 5, b * N:(b + 1) * N], X2[:, b * P:(b + 1) * P],
                                                           ident[0:N, 0:N])
                            turn.then_inc(X_turned, 1)
                        if c == 1 and i == 1:
                            turn_pair(0)
                        if c == 1 and i == 3:
                            pe.wait_ge(XT_out_v, 2 * layer + 2)
                            for b in range(KC):
                                times_qk(b, OTHER)
                            for b in range(JC):
                                times_qk(b, PAIR)
                    ins.then_inc(rel_done, 1)
                keep_warm(1, 5)
                turn_pair(1)
                pe.wait_ge(XT_out_s, layer + 1)
                for k in range(JC, KC):
                    ins = times_qk(k, PAIR)
                ins.then_inc(qk_done, 1)
                nc.tensor.matmul(ps[:, 0, 0:hp * n].rearrange("p (h c) -> p h c", h=hp), ident[:, :],
                                 maskb[:, :].unsqueeze(1).to_broadcast([P, hp, n]), start=True, stop=False,
                                 skip_group_check=True)
                pe.wait_ge(qkT_ready, layer + 1)
                for h in range(hp):
                    for half in range(2):
                        head = hp * half + h if hp == 2 else 0
                        rows = slice(half * N, (half + 1) * N)
                        nc.tensor.matmul(ps[rows, 0, h * n:(h + 1) * n],
                                         qsel[:, m // 2 + head:m // 2 + head + 1].to_broadcast([P, N]), QKT,
                                         start=False, stop=False, skip_group_check=True)
                for h in range(hp):
                    for r in range(R):
                        for half in range(2):
                            head = hp * half + h if hp == 2 else 0
                            ins = nc.tensor.matmul(ps[half * N:(half + 1) * N, 0, h * n + r * N:h * n + (r + 1) * N],
                                                   QKT[:, r * N:(r + 1) * N],
                                                   qsel[:, head:head + 1].to_broadcast([P, N]),
                                                   start=False, stop=True, skip_group_check=True)
                ins.then_inc(score_done, 1)
                ins = add_bias(f"L2_gnn_b{layer + 1}", ADDEND)
                if layer == 1:
                    ins = add_nodes(xa, ADDEND)
                ins.then_inc(addend_done, 1)
                keep_warm(9, 4)
                pe.wait_ge(wts_ready, 2 * layer + hp)
                for h in range(hp):
                    nc.tensor.transpose(ps[:, 3, h * P:(h + 1) * P], wts[:, h * n:h * n + P], ident[:, :])
                for h in range(hp):
                    ins = nc.tensor.transpose(ps[0:N, 7, h * P:(h + 1) * P], wts[:, h * n + P:(h + 1) * n], ident[:, :])
                ins.then_inc(wts_turned, 1)
                keep_warm(1, 4)
                pe.wait_ge(wT_out_v, layer + 1)
                pe.wait_ge(wT_out_s, layer + 1)
                for h in range(hp):
                    for half in range(2):
                        at = half * HD + h * bw
                        nc.tensor.matmul(ps[half * N:(half + 1) * N, ACC, h * bw:(h + 1) * bw],
                                         wT1[:, h * P + half * N:h * P + (half + 1) * N], X01[:, at:at + bw],
                                         start=True, stop=False, skip_group_check=True)
                        ins = nc.tensor.matmul(ps[half * N:(half + 1) * N, ACC, h * bw:(h + 1) * bw],
                                               wT2[:, h * P + half * N:h * P + (half + 1) * N], X2[:, at:at + bw],
                                               start=False, stop=True, skip_group_check=True)
                ins.then_inc(att_done, 1)
                if layer == 0:
                    keep_warm(8, 4)
            norm_stats(3, "L3_gnn_b1")
            gcn(6, "L3_W1", xa, (x_ready, 5), ACC)
            add_bias("L3_gnn_b2", LAST)
            keep_warm(1, 4)
            gcn(7, "L3_W2", hx, (y_ready, 1), LAST, xa)
            norm_stats(4)


def kernel(**inputs):
    import numpy as _np
    import concourse.bacc as _bacc
    from concourse import mybir as _mybir
    from concourse.bass_utils import run_bass_kernel_spmd as _run

    nc = _bacc.Bacc("TRN2", target_bir_lowering=False, num_devices=1)
    arrays, aps = {}, {}
    for name, value in inputs.items():
        v = _np.ascontiguousarray(value)
        arrays[f"in_{name}"] = v
        aps[name] = nc.dram_tensor(f"in_{name}", v.shape, _mybir.dt.from_np(v.dtype), kind="ExternalInput").ap()
    shape = arrays["in_x"].shape
    out = nc.dram_tensor("out", shape, _mybir.dt.float32, kind="ExternalOutput").ap()
    gnn_kernel(nc, aps, out)
    r = _run(nc, [arrays], core_ids=[0])
    return r.results[0]["out"]
```
